# Optimizing a Trainium2 kernel written in Bass

```python
import numpy as np
import jax
import jax.numpy as jnp

def _softmax(x, axis=-1):
    return jax.nn.softmax(x, axis=axis)

def _gelu(x):
    return jax.nn.gelu(x, approximate=True)

def _silu(x):
    return jax.nn.silu(x)

def _sigmoid(x):
    return jax.nn.sigmoid(x)

def _layernorm(x, axis=-1, eps=1e-05):
    m = jnp.mean(x, axis=axis, keepdims=True)
    v = jnp.var(x, axis=axis, keepdims=True)
    return (x - m) / jnp.sqrt(v + eps)

def _scatter_add(tgt, idx, src, axis=0):
    return tgt.at[idx].add(src)

def _segment_sum(src, seg, n):
    return jax.ops.segment_sum(src, seg, n)
kernel_name = 'mk_adaln_d1_jaxref_r8_47fcbb'

def setup_inputs(seed: int=0):
    np.random.seed(seed)
    _w = jnp.asarray

    def _L0_attn_setup():
        import math
        import jax, jax.numpy as jnp
        import numpy as np
        H = 32
        NOPE = 64
        ROPE = 64
        VD = 128
        QHD = NOPE + ROPE
        KVR = 32
        EPS = 1e-06

        def _yarn_cos_sin(seq_len, dim=ROPE, base=10000.0, factor=128.0, beta_fast=32.0, beta_slow=1.0, orig_max=1024, mscale=1.0, mscale_all_dim=1.0):

            def corr_dim(r):
                return dim * math.log(orig_max / (r * 2 * math.pi)) / (2 * math.log(base))
            low = max(math.floor(corr_dim(beta_fast)), 0)
            high = min(math.ceil(corr_dim(beta_slow)), dim - 1)
            hi = high + 0.001 if low == high else float(high)
            ramp = np.clip((np.arange(dim // 2, dtype=np.float32) - low) / (hi - low), 0.0, 1.0)
            inv_freq_mask = 1.0 - ramp
            freq_extra = 1.0 / base ** (np.arange(0, dim, 2, dtype=np.float32) / dim)
            freq_inter = freq_extra / factor
            inv_freq = freq_inter * (1.0 - inv_freq_mask) + freq_extra * inv_freq_mask
            t = np.arange(seq_len, dtype=np.float32)
            freqs = np.outer(t, inv_freq)
            emb = np.concatenate([freqs, freqs], axis=-1)

            def gm(s, m):
                return 1.0 if s <= 1 else 0.1 * m * math.log(s) + 1.0
            ms = gm(factor, mscale) / gm(factor, mscale_all_dim)
            return (jnp.asarray(np.cos(emb) * ms), jnp.asarray(np.sin(emb) * ms))

        def _rmsnorm(x, w, eps=EPS):
            var = jnp.mean(jnp.square(x), axis=-1, keepdims=True)
            return x * jax.lax.rsqrt(var + eps) * w

        def _deinterleave(x):
            d = x.shape[-1]
            x = x.reshape(*x.shape[:-1], d // 2, 2)
            return jnp.concatenate([x[..., 0], x[..., 1]], axis=-1)

        def _rotate_half(x):
            d = x.shape[-1] // 2
            return jnp.concatenate([-x[..., d:], x[..., :d]], axis=-1)

        def _apply_rope(x, cos, sin):
            return x * cos + _rotate_half(x) * sin
        key = jax.random.key(seed)
        ks = jax.random.split(key, 6)
        B, S, D = (1, 256, 512)
        std = 0.02
        return {'x': jax.random.normal(ks[0], (B, S, D), dtype=jnp.float32), 'wq_a': jax.random.normal(ks[1], (128, D), dtype=jnp.float32) * std, 'q_a_ln_w': jnp.ones((128,), dtype=jnp.float32), 'wq_b': jax.random.normal(ks[2], (H * QHD, 128), dtype=jnp.float32) * std, 'wkv_a': jax.random.normal(ks[3], (KVR + ROPE, D), dtype=jnp.float32) * std, 'kv_a_ln_w': jnp.ones((KVR,), dtype=jnp.float32), 'wkv_b': jax.random.normal(ks[4], (H * (NOPE + VD), KVR), dtype=jnp.float32) * std, 'wo': jax.random.normal(ks[5], (D, H * VD), dtype=jnp.float32) * std}
    _L0_attn_in = _L0_attn_setup()

    def _L0_ffn_setup():
        import jax, jax.numpy as jnp
        import numpy as np
        B, S, D, I = (4, 256, 512, 1376)

        def _dequant_matmul(x, w_int8, scale):
            w = w_int8.astype(x.dtype)
            return jnp.einsum('bsd,od->bso', x, w) * scale
        key = jax.random.key(seed)
        ks = jax.random.split(key, 7)
        x = jax.random.normal(ks[0], (B, S, D), dtype=jnp.float32)
        gate_w = jax.random.randint(ks[1], (I, D), -127, 128, dtype=jnp.int32)
        up_w = jax.random.randint(ks[2], (I, D), -127, 128, dtype=jnp.int32)
        down_w = jax.random.randint(ks[3], (D, I), -127, 128, dtype=jnp.int32)
        gate_s = jax.random.uniform(ks[4], (1,), dtype=jnp.float32) * 0.01 + 0.001
        up_s = jax.random.uniform(ks[5], (1,), dtype=jnp.float32) * 0.01 + 0.001
        down_s = jax.random.uniform(ks[6], (1,), dtype=jnp.float32) * 0.01 + 0.001
        return {'x': x, 'gate_w': gate_w, 'gate_s': gate_s, 'up_w': up_w, 'up_s': up_s, 'down_w': down_w, 'down_s': down_s}
    _L0_ffn_in = _L0_ffn_setup()
    _L0_c = _w((lambda *s: np.random.randn(*s).astype(np.float32) * 0.05)(1, 512))
    _L0_wmod = _w((lambda *s: np.random.randn(*s).astype(np.float32) * 0.05)(512, 6 * 512) * 512 ** (-0.5))
    _d = {'L0_attn_x': _L0_attn_in['x'], 'L0_attn_wq_a': _L0_attn_in['wq_a'], 'L0_attn_q_a_ln_w': _L0_attn_in['q_a_ln_w'], 'L0_attn_wq_b': _L0_attn_in['wq_b'], 'L0_attn_wkv_a': _L0_attn_in['wkv_a'], 'L0_attn_kv_a_ln_w': _L0_attn_in['kv_a_ln_w'], 'L0_attn_wkv_b': _L0_attn_in['wkv_b'], 'L0_attn_wo': _L0_attn_in['wo'], 'L0_ffn_gate_w': _L0_ffn_in['gate_w'], 'L0_ffn_gate_s': _L0_ffn_in['gate_s'], 'L0_ffn_up_w': _L0_ffn_in['up_w'], 'L0_ffn_up_s': _L0_ffn_in['up_s'], 'L0_ffn_down_w': _L0_ffn_in['down_w'], 'L0_ffn_down_s': _L0_ffn_in['down_s'], 'L0_c': _L0_c, 'L0_wmod': _L0_wmod}
    _x0 = _d['L0_attn_x']
    _d['L0_attn_x'] = jax.random.normal(jax.random.fold_in(jax.random.key(seed), 1), (1, 1024, 512), dtype=_x0.dtype)
    del _x0
    return _d

def reference(L0_attn_x, L0_attn_wq_a, L0_attn_q_a_ln_w, L0_attn_wq_b, L0_attn_wkv_a, L0_attn_kv_a_ln_w, L0_attn_wkv_b, L0_attn_wo, L0_ffn_gate_w, L0_ffn_gate_s, L0_ffn_up_w, L0_ffn_up_s, L0_ffn_down_w, L0_ffn_down_s, L0_c, L0_wmod):

    def _L0_attn_ref(x, wq_a, q_a_ln_w, wq_b, wkv_a, kv_a_ln_w, wkv_b, wo):
        import math
        import jax, jax.numpy as jnp
        import numpy as np
        H = 32
        NOPE = 64
        ROPE = 64
        VD = 128
        QHD = NOPE + ROPE
        KVR = 32
        EPS = 1e-06

        def _yarn_cos_sin(seq_len, dim=ROPE, base=10000.0, factor=128.0, beta_fast=32.0, beta_slow=1.0, orig_max=1024, mscale=1.0, mscale_all_dim=1.0):

            def corr_dim(r):
                return dim * math.log(orig_max / (r * 2 * math.pi)) / (2 * math.log(base))
            low = max(math.floor(corr_dim(beta_fast)), 0)
            high = min(math.ceil(corr_dim(beta_slow)), dim - 1)
            hi = high + 0.001 if low == high else float(high)
            ramp = np.clip((np.arange(dim // 2, dtype=np.float32) - low) / (hi - low), 0.0, 1.0)
            inv_freq_mask = 1.0 - ramp
            freq_extra = 1.0 / base ** (np.arange(0, dim, 2, dtype=np.float32) / dim)
            freq_inter = freq_extra / factor
            inv_freq = freq_inter * (1.0 - inv_freq_mask) + freq_extra * inv_freq_mask
            t = np.arange(seq_len, dtype=np.float32)
            freqs = np.outer(t, inv_freq)
            emb = np.concatenate([freqs, freqs], axis=-1)

            def gm(s, m):
                return 1.0 if s <= 1 else 0.1 * m * math.log(s) + 1.0
            ms = gm(factor, mscale) / gm(factor, mscale_all_dim)
            return (jnp.asarray(np.cos(emb) * ms), jnp.asarray(np.sin(emb) * ms))

        def _rmsnorm(x, w, eps=EPS):
            var = jnp.mean(jnp.square(x), axis=-1, keepdims=True)
            return x * jax.lax.rsqrt(var + eps) * w

        def _deinterleave(x):
            d = x.shape[-1]
            x = x.reshape(*x.shape[:-1], d // 2, 2)
            return jnp.concatenate([x[..., 0], x[..., 1]], axis=-1)

        def _rotate_half(x):
            d = x.shape[-1] // 2
            return jnp.concatenate([-x[..., d:], x[..., :d]], axis=-1)

        def _apply_rope(x, cos, sin):
            return x * cos + _rotate_half(x) * sin
        B, S, D = x.shape
        m = 0.1 * 1.0 * math.log(128.0) + 1.0
        softmax_scale = QHD ** (-0.5) * m * m
        q = _rmsnorm(x @ wq_a.T, q_a_ln_w) @ wq_b.T
        q = q.reshape(B, S, H, QHD)
        q_nope, q_pe = (q[..., :NOPE], q[..., NOPE:])
        ckv_kpe = x @ wkv_a.T
        ckv, k_pe = (ckv_kpe[..., :KVR], ckv_kpe[..., KVR:])
        kv = _rmsnorm(ckv, kv_a_ln_w) @ wkv_b.T
        kv = kv.reshape(B, S, H, NOPE + VD)
        k_nope, v = (kv[..., :NOPE], kv[..., NOPE:])
        cos, sin = _yarn_cos_sin(S)
        q_pe = _apply_rope(_deinterleave(q_pe), cos[None, :, None, :], sin[None, :, None, :])
        k_pe = _apply_rope(_deinterleave(k_pe), cos[None, :, :], sin[None, :, :])
        q_full = jnp.concatenate([q_nope, q_pe], axis=-1)
        k_full = jnp.concatenate([k_nope, jnp.broadcast_to(k_pe[:, :, None, :], (B, S, H, ROPE))], axis=-1)
        scores = jnp.einsum('bqhd,bkhd->bhqk', q_full, k_full) * softmax_scale
        causal = jnp.tril(jnp.ones((S, S), dtype=bool))
        scores = jnp.where(causal[None, None], scores, jnp.finfo(scores.dtype).min)
        attn = jax.nn.softmax(scores, axis=-1)
        out = jnp.einsum('bhqk,bkhd->bqhd', attn, v).reshape(B, S, H * VD)
        return out @ wo.T

    def _L0_ffn_ref(x, gate_w, gate_s, up_w, up_s, down_w, down_s):
        import jax, jax.numpy as jnp
        import numpy as np
        B, S, D, I = (4, 256, 512, 1376)

        def _dequant_matmul(x, w_int8, scale):
            w = w_int8.astype(x.dtype)
            return jnp.einsum('bsd,od->bso', x, w) * scale
        gate = jax.nn.silu(_dequant_matmul(x, gate_w, gate_s))
        up = _dequant_matmul(x, up_w, up_s)
        out = _dequant_matmul(gate * up, down_w, down_s)
        return out.astype(x.dtype)
    x = L0_attn_x
    mod = (_silu(L0_c) @ L0_wmod).reshape(L0_c.shape[0], 6, 1, -1)
    sa, ca, ga, sb, cb, gb = (mod[:, 0], mod[:, 1], mod[:, 2], mod[:, 3], mod[:, 4], mod[:, 5])
    ga = (2 * (ga >= 0) - 1) * jnp.maximum(jnp.abs(ga), 0.25)
    gb = (2 * (gb >= 0) - 1) * jnp.maximum(jnp.abs(gb), 0.25)
    h = _layernorm(x, axis=-1) * (1 + ca) + sa
    x = x + ga * _L0_attn_ref(h, L0_attn_wq_a, L0_attn_q_a_ln_w, L0_attn_wq_b, L0_attn_wkv_a, L0_attn_kv_a_ln_w, L0_attn_wkv_b, L0_attn_wo)
    h = _layernorm(x, axis=-1) * (1 + cb) + sb
    x = x + gb * _L0_ffn_ref(h, L0_ffn_gate_w, L0_ffn_gate_s, L0_ffn_up_w, L0_ffn_up_s, L0_ffn_down_w, L0_ffn_down_s)
    return x

_drawn_inputs = setup_inputs


def setup_inputs(seed=0):
    import zlib

    import numpy as np

    out = dict(_drawn_inputs(seed))
    spreads = {'L0_attn_q_a_ln_w': (1.0, 0.6), 'L0_attn_kv_a_ln_w': (1.0, 0.6)}
    factors = {'L0_attn_wq_a': 8.0,
     'L0_attn_wq_b': 8.0,
     'L0_attn_wkv_a': 8.0,
     'L0_attn_wkv_b': 8.0,
     'L0_attn_wo': 8.0}
    for name, (base, spread) in spreads.items():
        noise = np.random.default_rng([zlib.crc32(name.encode()), seed]).standard_normal(out[name].shape)
        drawn = base * np.exp(spread * noise) if base else spread * noise
        out[name] = jnp.asarray(drawn.astype(out[name].dtype))
    for name, factor in factors.items():
        out[name] = (out[name] * factor).astype(out[name].dtype)
    return out
```

```python
import concourse.bass as bass
from concourse import mybir
from concourse.alu_op_type import AluOpType as ALU
from contextlib import ExitStack, contextmanager
import math
import numpy as np

F32 = mybir.dt.float32
F32R = mybir.dt.float32r
BF16 = mybir.dt.bfloat16
I32 = mybir.dt.int32
ACT = mybir.ActivationFunctionType
AX = mybir.AxisListType

P = 128
S, D, H = 1024, 512, 32
R, L, HALF = 128, 32, 32
NOPE, VD = 64, 128
I = 1376
G, HG = 8, 4
KR = 2 * HALF + L
KD = D // P
NS = S // P
QB = 512
NQB = S // QB
NC, IT = I // P, I % P
EPS_RMS, EPS_LN = 1e-6, 1e-5
FLOOR = 0.25
MASKED = -1e30
STEPS = [(qb, kt) for qb in range(NQB) for kt in range((qb + 1) * QB // P)]
NSTEP = len(STEPS)


def softmax_scale():
    m = 0.1 * math.log(128.0) + 1.0
    return (NOPE + 2 * HALF) ** -0.5 * m * m


def width(qb, kt):
    return min(QB, (qb + 1) * QB - kt * P)


class Count:

    def __init__(self, handle):
        self.h, self.n = handle, 0

    def inc(self, ins, k=1):
        ins.then_inc(self.h, k)
        self.n += k
        return self.n


def build(nc, t, out):
    pe, act, dve, pool, sp = nc.tensor, nc.scalar, nc.vector, nc.gpsimd, nc.sync
    top = ExitStack()
    with top:
        def sem(name):
            return Count(top.enter_context(nc.semaphore(name)))

        def sb(name, shape, dt=F32, where=top):
            return where.enter_context(nc.sbuf_tensor(name, shape, dt))

        s_seen = [sem("s_seen_pool"), sem("s_seen_sp")]

        def wait(eng, s, value):
            eng.wait_ge(s.h, value)
            if not isinstance(value, int) and eng in (sp, pool):
                eng.sem_inc(s_seen[eng is sp].h, 1)

        PS = top.enter_context(nc.psum_tensor("PS", [P, 8, 512], F32))
        ident = sb("ident", [P, P])
        ones = sb("ones", [P, P])
        gate_a = sb("gate_a", [P, D])
        gate_b = sb("gate_b", [P, D])
        lnq = sb("lnq", [P, 1])
        lnkv = sb("lnkv", [P, 1])
        ffn_s = sb("ffn_s", [P, 3])
        mod_col = sb("mod_col", [P, 4, KD])
        eps = sb("eps", [P, 2])
        stats = sb("stats", [P, NS, 6])
        mv = sb("mv", [P, NS, 2])
        rstd = sb("rstd", [P, NS])
        wide = sb("wide", [P, NC, S])
        attn = wide[:, 0:G, :]

        s_const, s_small, s_x = sem("s_const"), sem("s_small"), sem("s_x")
        s_out = sem("s_out")

        def barrier():
            nc.all_engine_barrier()

        s_const.inc(pool.memset(ident[:], 0.0))
        s_const.inc(pool.memset(ones[:], 1.0))
        s_const.inc(pool.memset(eps[:, 0:1], EPS_RMS))
        s_const.inc(pool.memset(eps[:, 1:2], EPS_LN))
        wait(pool, s_const, 4)
        s_const.inc(pool.affine_select(out=ident[:], in_=ident[:], compare_op=ALU.not_equal, fill=1.0,
                                       base=0, pattern=[[-1, P]], channel_multiplier=1))

        with ExitStack() as shared:
            KH = sb("KH", [P, S], F32R, shared)
            KL = sb("KL", [P, S], F32R, shared)
            V = sb("V", [P, NS, L], F32, shared)
            QNH = sb("QNH", [P, S], F32R, shared)
            QNL = sb("QNL", [P, S], F32R, shared)
            cos = sb("cos", [P, S], F32, shared)
            sin = sb("sin", [P, S], F32, shared)

            with ExitStack() as c:
                phase_inputs(nc, t, c, sb, sem, wait, locals())
            barrier()
            with ExitStack() as c:
                phase_attention(nc, t, c, sb, sem, wait, locals())
            barrier()
        x1 = sb("x1", [P, NS, D])
        h2H = sb("h2H", [P, KD, S], F32R)
        h2L = sb("h2L", [P, KD, S], F32R)
        with ExitStack() as c:
            phase_project(nc, t, c, sb, sem, wait, locals())
        barrier()
        with ExitStack() as c:
            phase_ffn(nc, t, c, sb, sem, wait, locals(), out)


def normalise_transpose(nc, c, sb, sem, wait, tag, x, ready, mod, outH, outL, sh):
    pe, act, dve, pool = nc.tensor, nc.scalar, nc.vector, nc.gpsimd
    PS, ident, mv, stats, rstd, mod_col, eps = (sh[k] for k in ("PS", "ident", "mv", "stats", "rstd", "mod_col", "eps"))
    xn = sb("xn" + tag, [P, NS, D], F32, c)
    full = sb("hfull" + tag, [P, 2, 512], F32, c)
    s_mv, s_sq, s_rs, s_xn, s_tr, s_full, s_hi, s_lo = (sem(n + tag) for n in (
        "s_mv", "s_sq", "s_rs", "s_xn", "s_tr", "s_full", "s_hi", "s_lo"))
    for st in range(NS):
        ready(dve, st)
        s_mv.inc(dve.bn_stats(stats[:, st, :], x[:, st, :]))
        wait(dve, s_mv, s_mv.n)
        s_mv.inc(dve.bn_aggr(mv[:, st, :], stats[:, st, :]))
        if st % 4 == 3:
            half = slice(st - 3, st + 1)
            wait(act, s_mv, s_mv.n)
            s_sq.inc(act.activation(rstd[:, half], mv[:, half, 1], ACT.Sqrt, bias=eps[:, 1:2]))
            wait(dve, s_sq, s_sq.n)
            s_rs.inc(dve.reciprocal(rstd[:, half], rstd[:, half]))
            wait(dve, s_rs, s_rs.n)
            for k in range(st - 3, st + 1):
                s_xn.inc(dve.tensor_scalar(xn[:, k, :], x[:, k, :], mv[:, k, 0:1], rstd[:, k:k + 1],
                                           ALU.subtract, ALU.mult))
    for n in range(2 * KD):
        hf, d = divmod(n, KD)
        wait(pe, s_xn, 4 * (hf + 1))
        for k in range(4):
            ins = pe.transpose(PS[:, n, k * P:(k + 1) * P], xn[:, 4 * hf + k, d * P:(d + 1) * P], ident[:])
        s_tr.inc(ins)
        cols = slice(hf * 512, hf * 512 + 512)
        wait(act, s_tr, s_tr.n)
        mod(act)
        if n >= 2:
            wait(act, s_lo, n - 1)
        s_full.inc(act.activation(full[:, n % 2, :], PS[:, n, :], ACT.Identity,
                                  scale=mod_col[:, sh["which"], d:d + 1], bias=mod_col[:, sh["which"] + 1, d:d + 1]))
        wait(dve, s_full, n + 1)
        s_hi.inc(dve.tensor_copy(outH[:, d, cols], full[:, n % 2, :]))
        wait(pool, s_hi, n + 1)
        s_lo.inc(pool.tensor_tensor(outL[:, d, cols], full[:, n % 2, :], outH[:, d, cols].bitcast(F32), ALU.subtract))
    return s_hi, s_lo, s_tr, s_full


def phase_inputs(nc, t, c, sb, sem, wait, sh):
    pe, act, dve, pool, sp = nc.tensor, nc.scalar, nc.vector, nc.gpsimd, nc.sync
    g = lambda k: sh[k]
    PS, ident, ones, KH, KL, V, QNH, QNL, cos, sin = map(g, ("PS", "ident", "ones", "KH", "KL", "V", "QNH", "QNL", "cos", "sin"))
    gate_a, gate_b, lnq, lnkv, ffn_s, mod_col, eps = map(g, (
        "gate_a", "gate_b", "lnq", "lnkv", "ffn_s", "mod_col", "eps"))
    s_const, s_small = g("s_const"), g("s_small")
    x = sb("x_in", [P, NS, D], F32, c)
    cT = sb("cT", [P, 3, KD], F32, c)
    wm = sb("wm", [P, 2, KD, D], F32, c)
    WA = sb("WA", [P, KD, R + KR + 2 * HALF], F32, c)
    WAH = sb("WAH", [P, KD, R + KR + 2 * HALF], F32R, c)
    WAL = sb("WAL", [P, KD, R + KR + 2 * HALF], F32R, c)
    hH = sb("hH", [P, KD, S], F32R, c)
    hL = sb("hL", [P, KD, S], F32R, c)
    tmp = sb("tmp", [P, 3, 512], F32, c)
    swap_sin = sb("swap_sin", [2 * HALF, S], F32, c)
    KF = sb("KF", [P, S], F32, c)
    scb = sb("scb", [P, KD, P], F32, c)

    s_xt = [sem(f"s_xt{i}") for i in range(NS)]
    s_wm = [sem(f"s_wm{i}") for i in range(6)]
    s_wa, s_rope = sem("s_wa"), sem("s_rope")
    s_small.inc(sp.dma_start(cT[:, 0, :], t["c"]), 16)
    xt = t["x"].rearrange("(n p) d -> p n d", p=P)
    for st in range(NS):
        s_xt[st].inc(act.dma_start(x[:, st, :], xt[:, st, :]), 16)
    for b, k in enumerate((1, 0)):
        s_wm[b].inc(sp.dma_start(wm[:, b, :, :], t["wmod"][k]), 16)
    s_wa.inc(sp.dma_start(WA[:], t["wa"]), 16)
    s_small.inc(sp.dma_start(lnq[:], t["lnq"]), 16)
    s_small.inc(sp.dma_start(lnkv[2 * HALF:KR, :], t["lnkv"]), 16)
    s_small.inc(sp.dma_start(ffn_s[:], t["ffn_s"]), 16)
    s_rope.inc(sp.dma_start(cos[:], t["cos"]), 16)
    s_rope.inc(sp.dma_start(sin[:], t["sin"]), 16)
    s_rope.inc(sp.dma_start(swap_sin[:], t["swap_sin"]), 16)

    s_c = sem("s_c")
    wait(act, s_small, 64)
    s_c.inc(act.activation(cT[:, 1, :], cT[:, 0, :], ACT.Silu))
    wait(dve, s_small, 64)
    wait(dve, s_const, 5)
    dve.tensor_scalar(lnq[:], lnq[:], softmax_scale(), None, ALU.mult)
    wait(dve, s_c, 1)
    for k in range(KD):
        last = dve.tensor_scalar(scb[:, k, :], ones[:], cT[:, 1, k:k + 1], None, ALU.mult)
    s_scb = sem("s_scb")
    s_scb.inc(last)

    s_m, s_mc = sem("s_m"), sem("s_mc")
    ORDER = [1, 0, 4, 3, 2, 5]
    wait(pe, s_const, 5)
    wait(pe, s_scb, 1)
    for n, which in enumerate(ORDER):
        b = n % 2
        if n >= 2:
            wait(sp, s_m, n - 1)
            s_wm[n].inc(sp.dma_start(wm[:, b, :, :], t["wmod"][which]), 16)
        wait(pe, s_wm[n], 16)
        if n < 4:
            for d in range(KD):
                for k in range(KD):
                    ins = pe.matmul(PS[:, 7, 8 * n + d:8 * n + d + 1], wm[:, b, k, d * P:(d + 1) * P], cT[:, 1, k:k + 1],
                                    start=(k == 0), stop=(k == KD - 1))
            s_m.inc(ins)
            wait(dve, s_m, n + 1)
            dst = mod_col[:, n, :]
            src = PS[:, 7, 8 * n:8 * n + KD]
            s_mc.inc(dve.tensor_scalar(dst, src, 1.0 if n % 2 == 0 else 0.0, None, ALU.add))
            wait(pe, s_mc, n + 1)
        else:
            for k in range(KD):
                ins = pe.matmul(PS[:, n, :], scb[:, k, :], wm[:, b, k, :], start=(k == 0), stop=(k == KD - 1))
            s_m.inc(ins)
            wait(dve, s_m, n + 1)
            s_mc.inc(dve.tensor_copy(tmp[:, 0, :], PS[:, n, :]))
            wait(dve, s_mc, s_mc.n)
            dst = gate_a if n == 4 else gate_b
            s_mc.inc(dve.tensor_scalar(tmp[:, 1, :], tmp[:, 0, :], -1.0, None, ALU.mult))
            wait(dve, s_mc, s_mc.n)
            s_mc.inc(dve.tensor_tensor(tmp[:, 1, :], tmp[:, 0, :], tmp[:, 1, :], ALU.max))
            wait(dve, s_mc, s_mc.n)
            s_mc.inc(dve.tensor_scalar(tmp[:, 1, :], tmp[:, 1, :], FLOOR, None, ALU.max))
            s_mc.inc(dve.tensor_scalar(tmp[:, 0, :], tmp[:, 0, :], 0.0, 2.0, ALU.is_ge, ALU.mult))
            wait(dve, s_mc, s_mc.n)
            s_mc.inc(dve.scalar_tensor_tensor(out=dst[:], in0=tmp[:, 0, :], scalar=-1.0, in1=tmp[:, 1, :],
                                              op0=ALU.add, op1=ALU.mult))
            wait(pe, s_mc, s_mc.n)
            wait(dve, s_mc, s_mc.n)

    s_wah = sem("s_wah")
    wait(act, s_wa, 16)
    s_wah.inc(act.activation(WAH[:], WA[:], ACT.Copy))
    wait(pool, s_wah, 1)
    s_wal = sem("s_wal")
    s_wal.inc(pool.tensor_tensor(WAL[:], WA[:], WAH[:].bitcast(F32), ALU.subtract))

    s_hi, s_lo, s_tr, s_full = normalise_transpose(
        nc, c, sb, sem, wait, "1", x, lambda e, st: wait(e, s_xt[st], 16), lambda e: wait(e, s_mc, 4), hH, hL,
        dict(sh, which=0))

    s_pj, s_sq, s_ss, s_rt, s_inv, s_kv = (sem(n) for n in ("s_pj", "s_sqr", "s_ss", "s_rt", "s_inv", "s_kv"))
    s_ev = sem("s_ev")
    wait(pe, s_wal, 1)
    wait(pe, s_full, 2 * KD)
    for hf in range(2):
        cols = slice(hf * 512, hf * 512 + 512)
        wait(pe, s_lo, KD * (hf + 1))
        for bank, lo, m in ((hf, 0, R), (2 + hf, R, KR), (4 + hf, R + KR, 2 * HALF)):
            for n, (w, h) in enumerate(((WAH, hH), (WAL, hH), (WAH, hL))):
                for k in range(KD):
                    ins = pe.matmul(PS[0:m, bank, :], w[:, k, lo:lo + m], h[:, k, cols],
                                    start=(n == 0 and k == 0), stop=(n == 2 and k == KD - 1))
            s_pj.inc(ins)
    lat = slice(2 * HALF, KR)
    rot = slice(0, 2 * HALF)
    wait(dve, s_rope, 48)
    for hf in range(2):
        cols = slice(hf * 512, hf * 512 + 512)
        wait(act, s_pj, 3 * hf + 1)
        if hf:
            wait(act, s_kv, 1)
        s_sq.inc(act.activation(tmp[:, 0, :], PS[:, hf, :], ACT.Square))
        wait(act, s_pj, 3 * hf + 2)
        s_sq.inc(act.activation(tmp[lat, 1, :], PS[lat, 2 + hf, :], ACT.Square))
        wait(pe, s_sq, 2 * hf + 1)
        if hf:
            wait(pe, s_rt, 2)
        s_ss.inc(pe.matmul(PS[:, 6, :], ones[:], tmp[:, 0, :], start=True, stop=True))
        wait(pe, s_sq, 2 * hf + 2)
        s_ss.inc(pe.matmul(PS[lat, 7, :], ones[lat, 0:L], tmp[lat, 1, :], start=True, stop=True))
        wait(act, s_ss, 2 * hf + 1)
        s_rt.inc(act.activation(tmp[:, 0, :], PS[:, 6, :], ACT.Sqrt, scale=1.0 / R, bias=eps[:, 0:1]))
        wait(act, s_ss, 2 * hf + 2)
        s_rt.inc(act.activation(tmp[lat, 1, :], PS[lat, 7, :], ACT.Sqrt, scale=1.0 / L, bias=eps[lat, 0:1]))
        wait(dve, s_rt, 2 * hf + 1)
        s_inv.inc(dve.reciprocal(tmp[:, 0, :], tmp[:, 0, :]))
        wait(dve, s_rt, 2 * hf + 2)
        s_inv.inc(dve.reciprocal(tmp[lat, 1, :], tmp[lat, 1, :]))
        wait(dve, s_inv, 2 * hf + 2)
        if hf:
            wait(dve, s_kv, 2)
        s_ev.inc(dve.tensor_tensor(tmp[:, 2, :], PS[:, hf, :], tmp[:, 0, :], ALU.mult))
        wait(dve, s_ev, s_ev.n)
        s_ev.inc(dve.tensor_copy(QNH[:, cols], tmp[:, 2, :]))
        wait(dve, s_ev, s_ev.n)
        s_ev.inc(dve.tensor_tensor(QNL[:, cols], tmp[:, 2, :], QNH[:, cols].bitcast(F32), ALU.subtract))
        s_ev.inc(dve.scalar_tensor_tensor(out=KF[lat, cols], in0=PS[lat, 2 + hf, :], scalar=lnkv[lat, :],
                                          in1=tmp[lat, 1, :], op0=ALU.mult, op1=ALU.mult))
        wait(dve, s_ev, s_ev.n)
        s_ev.inc(dve.tensor_tensor(tmp[rot, 2, :], PS[rot, 2 + hf, :], cos[rot, cols], ALU.mult))
        wait(dve, s_pj, 3 * hf + 3)
        s_ev.inc(dve.tensor_tensor(tmp[rot, 0, :], PS[rot, 4 + hf, :], swap_sin[:, cols], ALU.mult))
        wait(dve, s_ev, s_ev.n)
        s_kv.inc(dve.tensor_tensor(KF[rot, cols], tmp[rot, 2, :], tmp[rot, 0, :], ALU.add))
        wait(dve, s_kv, s_kv.n)
        s_kv.inc(dve.tensor_copy(KH[0:KR, cols], KF[0:KR, cols]))
        wait(dve, s_kv, s_kv.n)
        s_kv.inc(dve.tensor_tensor(KL[0:KR, cols], KF[0:KR, cols], KH[0:KR, cols].bitcast(F32), ALU.subtract))
    s_k1 = sem("s_k1")
    s_k1.inc(dve.memset(KH[KR:KR + 1, :].bitcast(F32), 1.0))
    wait(pe, s_kv, 6)
    wait(pe, s_inv, 4)
    wait(pe, s_rt, 4)
    for kt in range(NS):
        ins = pe.transpose(PS[:, 6, kt * L:(kt + 1) * L], KF[lat, kt * P:(kt + 1) * P], ident[lat, lat])
    s_v = sem("s_v")
    s_v.inc(ins)
    wait(dve, s_v, 1)
    s_k1.inc(dve.tensor_copy(V[:].rearrange("p n l -> p (n l)"), PS[:, 6, 0:NS * L]))
    wait(dve, s_k1, 2)


def phase_attention(nc, t, c, sb, sem, wait, sh):
    pe, act, dve, pool, sp = nc.tensor, nc.scalar, nc.vector, nc.gpsimd, nc.sync
    g = lambda k: sh[k]
    PS, ident, ones, KH, KL, V, QNH, QNL, cos, sin = map(g, ("PS", "ident", "ones", "KH", "KL", "V", "QNH", "QNL", "cos", "sin"))
    lnq, attn = g("lnq"), g("attn")
    Q = sb("Q", [P, 2, 2, HG, S], F32R, c)
    WP = sb("WP", [P, 2 * P], F32, c)
    WN = sb("WN", [NOPE, HG, R], F32, c)
    WK = sb("WK", [NOPE, HG, L], F32, c)
    WF = sb("WF", [P, 3 * P], F32, c)
    WH = sb("WH", [P, 3 * P], F32R, c)
    WL = sb("WL", [P, 3 * P], F32R, c)
    RT = sb("RT", [P, 4, 512], F32, c)
    RE = sb("RE", [P, 2, 512], F32, c)
    TQ = sb("TQ", [P, 2, 3, 2, 512], F32R, c)
    PR = sb("PR", [P, 3, HG, QB], F32, c)
    NMa = sb("NMa", [P, HG, NS], F32, c)
    NMb = sb("NMb", [P, HG, NS // 2], F32, c)
    NM = sb("NM", [HG * NS, P], F32R, c)
    RD = sb("RD", [P, QB], F32, c)
    identb = sb("identb", [P, P], BF16, c)
    maskb = sb("maskb", [P, P], BF16, c)

    s_w = sem("s_w")
    s_wf = sem("s_wf")
    s_wh = sem("s_wh")
    s_wl = sem("s_wl")
    s_af = sem("s_af")
    s_ar = sem("s_ar")
    s_re = sem("s_re")
    s_th = sem("s_th")
    s_tl = sem("s_tl")
    s_q = [sem("s_q0"), sem("s_q1")]
    s_nm = sem("s_nm")
    s_nd = sem("s_nd")
    s_st = sem("s_st")
    s_p = sem("s_p")
    s_pv = sem("s_pv")
    s_o = sem("s_o")
    s_rd = sem("s_rd")
    s_mk = sem("s_mk")
    UNITS = 1 + 6 + 12 * HG + 1
    NPAIR = 2 * NSTEP

    s_mk.inc(pool.memset(identb[:], 0.0))
    s_mk.inc(pool.memset(maskb[:], 0.0))
    wait(pool, s_mk, 2)
    s_mk.inc(pool.affine_select(out=identb[:], in_=identb[:], compare_op=ALU.not_equal, fill=1.0, base=0,
                                pattern=[[-1, P]], channel_multiplier=1))
    s_mk.inc(pool.affine_select(out=maskb[:], in_=maskb[:], compare_op=ALU.is_ge, fill=MASKED, base=0,
                                pattern=[[-1, P]], channel_multiplier=1))
    wait(pe, s_mk, 4)
    dve.sem_inc(s_ar.h, 2)
    dve.sem_inc(s_o.h, 1)
    act.sem_inc(s_p.h, 2)
    pe.sem_inc(s_pv.h, 3)

    def load_weights(grp):
        s_w.inc(sp.dma_start(WP[:], t["wq_pe"][bass.ds(grp, 1)].rearrange("g p n -> (g p) n")), 16)
        s_w.inc(sp.dma_start(WN[:].rearrange("p h r -> p (h r)"),
                             t["wq_nope"][bass.ds(grp, 1)].rearrange("g p n -> (g p) n")), 16)
        s_w.inc(sp.dma_start(WK[:].rearrange("p h r -> p (h r)"),
                             t["wk"][bass.ds(grp, 1)].rearrange("g p n -> (g p) n")), 16)

    def side_units(grp, par):
        first = UNITS * grp
        work = []

        def bank(u):
            return PS[:, 6 + u % 2, :]

        def begin(u):
            wait(pe, s_ar, first + u + 1)

        def weights_pe():
            begin(0)
            wait(pe, s_w, 48 * (grp + 1))
            for h in range(HG):
                ins = pe.matmul(bank(0)[:, h * L:(h + 1) * L], WN[:, h, :], WK[:, h, :], start=True, stop=True)
            s_af.inc(ins)
            wait(dve, s_w, 48 * (grp + 1))
            wait(dve, s_wh, grp)
            wait(dve, s_wl, grp)
            s_wf.inc(dve.tensor_scalar(WF[:, 0:2 * P], WP[:], lnq[:], None, ALU.mult))
            wait(dve, s_af, first + 1)
            ins = dve.tensor_scalar(WF[:, 2 * P:], bank(0)[:, 0:HG * L], lnq[:], None, ALU.mult)
            s_ar.inc(ins)

        def weights_split():
            wait(act, s_wf, grp + 1)
            wait(act, s_ar, 2 + first + 1)
            wait(act, s_af, first)
            s_wh.inc(act.activation(WH[:], WF[:], ACT.Copy))
            wait(pool, s_wh, grp + 1)
            s_wl.inc(pool.tensor_tensor(WL[:], WF[:], WH[:].bitcast(F32), ALU.subtract))

        def project(u, block, hf):
            cols = slice(hf * 512, hf * 512 + 512)
            begin(u)
            wait(pe, s_wl, grp + 1)
            for n, (w, q) in enumerate(((WH, QNH), (WL, QNH), (WH, QNL))):
                ins = pe.matmul(bank(u), w[:, block * P:(block + 1) * P], q[:, cols], start=(n == 0), stop=(n == 2))
            s_af.inc(ins)

        def rotary(hf):
            cols = slice(hf * 512, hf * 512 + 512)
            u = 1 + 3 * hf
            half = 2 * grp + hf
            project(u, 0, hf)
            project(u + 1, 1, hf)
            wait(dve, s_af, first + u + 1)
            wait(dve, s_re, 2 * half)
            dve.tensor_tensor(RT[:, 0, :], bank(u), cos[:, cols], ALU.mult)
            s_ar.inc(dve.tensor_tensor(RT[:, 3, :], bank(u), sin[:, cols], ALU.mult))
            wait(dve, s_af, first + u + 2)
            dve.tensor_tensor(RT[:, 1, :], bank(u + 1), sin[:, cols], ALU.mult)
            ins = dve.tensor_tensor(RT[:, 2, :], bank(u + 1), cos[:, cols], ALU.mult)
            s_ar.inc(ins)
            wait(pool, s_ar, 2 + first + u + 2)
            wait(pool, s_tl, half)
            s_re.inc(pool.tensor_tensor(RE[:, 0, :], RT[:, 0, :], RT[:, 1, :], ALU.subtract))
            s_re.inc(pool.tensor_tensor(RE[:, 1, :], RT[:, 2, :], RT[:, 3, :], ALU.add))

        def split(hf):
            u = 3 + 3 * hf
            half = 2 * grp + hf
            project(u, 2, hf)
            wait(act, s_q[hf], 192 * grp)
            wait(act, s_re, 2 * half + 2)
            s_th.inc(act.activation(TQ[:, hf, 0:2, 0, :], RE[:], ACT.Copy))
            wait(act, s_af, first + u + 1)
            s_th.inc(act.activation(TQ[:, hf, 2, 0, :], bank(u), ACT.Copy))
            wait(dve, s_th, 2 * half + 2)
            s_ar.inc(dve.tensor_tensor(TQ[:, hf, 2, 1, :], bank(u), TQ[:, hf, 2, 0, :].bitcast(F32), ALU.subtract))
            wait(pool, s_th, 2 * half + 1)
            s_tl.inc(pool.tensor_tensor(TQ[:, hf, 0:2, 1, :], RE[:], TQ[:, hf, 0:2, 0, :].bitcast(F32), ALU.subtract))
            wait(sp, s_ar, first + u + 1 + 2)
            wait(sp, s_tl, half + 1)
            for h in range(HG):
                for b in range(3):
                    s_q[hf].inc(sp.dma_start(
                        Q[b * 32:(b + 1) * 32, par, :, h, hf * 512:(hf + 1) * 512].bitcast(F32),
                        TQ[h * 32:(h + 1) * 32, hf, b, :, :].bitcast(F32)), 16)

        order = [(h, qt, 0) for qt in range(NS // 2) for h in range(HG)]
        order += [(h, qt, part) for qt in range(NS // 2, NS) for h in range(HG) for part in range(2)]

        def max_unit(u, h, qt, part):
            begin(u)
            wait(pe, s_q[qt * P // 512], 192 * (grp + 1))
            lo = part * 512
            n = min(512, (qt + 1) * P - lo)
            diagonal = (qt + 1) * P == lo + n
            ins = pe.matmul(bank(u)[:, 0:n], Q[0:KR, par, 0, h, qt * P:(qt + 1) * P], KH[0:KR, lo:lo + n],
                            start=True, stop=not diagonal)
            if diagonal:
                ins = pe.matmul(bank(u)[:, n - P:n], identb[:], maskb[:], start=False, stop=True)
            s_af.inc(ins)
            wait(dve, s_af, first + u + 1)
            dst = NMb[:, h, qt - NS // 2:qt - NS // 2 + 1] if part else NMa[:, h, qt:qt + 1]
            s_ar.inc(dve.tensor_reduce(dst, bank(u)[:, 0:n], axis=AX.X, op=ALU.max, negate=True))

        def rows():
            wait(dve, s_ar, 2 + first + UNITS - 1)
            s_nm.inc(dve.tensor_tensor(NMa[:, :, NS // 2:], NMa[:, :, NS // 2:], NMb[:], ALU.min))
            begin(UNITS - 1)
            wait(pe, s_nm, grp + 1)
            s_af.inc(pe.transpose(bank(UNITS - 1)[0:HG * NS, 0:P], NMa[:].rearrange("p h n -> p (h n)"), ident[:]))
            wait(dve, s_af, first + UNITS)
            wait(dve, s_nd, 16 * grp)
            ins = dve.tensor_copy(NM[:], bank(UNITS - 1)[0:HG * NS, 0:P])
            s_ar.inc(ins)
            wait(sp, s_ar, 2 + first + UNITS)
            s_nd.inc(sp.dma_start(Q[KR:KR + 1, par, 0, :, :].rearrange("p h (n q) -> p (h n) q", q=P).bitcast(F32),
                                  NM[:].bitcast(F32)), 16)

        work = [(0, weights_pe), (1, weights_split), (2, lambda: rotary(0)), (3, lambda: split(0)),
                (3, lambda: rotary(1)), (4, lambda: split(1))]
        for n, (h, qt, part) in enumerate(order):
            step = 4 if n < 3 else 5 + (n - 3) * 5 // (len(order) - 3)
            work.append((step, lambda u=7 + n, h=h, qt=qt, part=part: max_unit(u, h, qt, part)))
        work.append((10, rows))
        return work

    def scores(grp, par, s):
        qb, kt = STEPS[s]
        w = width(qb, kt)
        q0 = (qb + 1) * QB - w
        diagonal = kt * P >= qb * QB
        for p in range(2):
            pair = NPAIR * grp + 2 * s + p
            wait(pe, s_p, pair + 1)
            if s == 0 and p == 0:
                wait(pe, s_nd, 16 * (grp + 1))
            for h in (2 * p, 2 * p + 1):
                dst = PS[:, h, 0:w]
                ks = slice(kt * P, (kt + 1) * P)
                pe.matmul(dst, KH[0:KR + 1, ks], Q[0:KR + 1, par, 0, h, q0:q0 + w], start=True, stop=False)
                pe.matmul(dst, KL[0:KR, ks], Q[0:KR, par, 0, h, q0:q0 + w], start=False, stop=False)
                ins = pe.matmul(dst, KH[0:KR, ks], Q[0:KR, par, 1, h, q0:q0 + w], start=False, stop=not diagonal)
                if diagonal:
                    ins = pe.matmul(PS[:, h, 0:P], maskb[:], identb[:], start=False, stop=True)
            s_st.inc(ins)
            wait(act, s_st, pair + 1)
            wait(act, s_pv, NSTEP * grp + s + 1)
            s_p.inc(act.activation(PR[:, s % 3, 2 * p:2 * p + 2, 0:w], PS[:, 2 * p:2 * p + 2, 0:w], ACT.Exp))

    def values(grp, s):
        qb, kt = STEPS[s]
        w = width(qb, kt)
        wait(pe, s_p, 2 + NPAIR * grp + 2 * s + 2)
        if kt == 0:
            wait(pe, s_o, 1 + 2 * grp + qb)
        last = kt == (qb + 1) * QB // P - 1
        for bank, of in ((4, V[:, kt, :]), (5, ones[:, 0:L])):
            for h in range(HG):
                ins = pe.matmul(PS[h * L:(h + 1) * L, bank, QB - w:QB], of, PR[:, s % 3, h, 0:w],
                                start=(kt == 0), stop=last)
        s_pv.inc(ins)

    def store(grp, qb):
        wait(dve, s_pv, 3 + NSTEP * grp + (4 if qb == 0 else NSTEP))
        s_rd.inc(dve.reciprocal(RD[:], PS[:, 5, :]))
        wait(dve, s_rd, 2 * grp + qb + 1)
        s_o.inc(dve.tensor_tensor(attn[:, bass.ds(grp, 1), qb * QB:(qb + 1) * QB].rearrange("p g q -> p (g q)"),
                                  PS[:, 4, :], RD[:], ALU.mult))

    def window(grp, par, side):
        if side:
            wait(sp, s_wf, grp + 1)
            wait(sp, s_af, UNITS * grp + 1)
            load_weights(grp + 1)
        work = side_units(grp + 1, 1 - par) if side else []
        for s in range(NSTEP):
            scores(grp, par, s)
            if s > 0:
                values(grp, s - 1)
            if s == 4:
                store(grp, 0)
            for step, f in work:
                if step == s:
                    f()
        values(grp, NSTEP - 1)
        store(grp, 1)

    load_weights(0)
    for step, f in side_units(0, 0):
        f()
    with nc.Fori(0, (G - 2) // 2) as i:
        window(2 * i, 0, True)
        window(2 * i + 1, 1, True)
    window(G - 2, 0, True)
    window(G - 1, 1, False)
    for e in (act, pe):
        wait(e, s_o, 1 + 2 * G)
    wait(sp, s_nd, 16 * G)


def phase_project(nc, t, c, sb, sem, wait, sh):
    pe, act, dve, pool, sp = nc.tensor, nc.scalar, nc.vector, nc.gpsimd, nc.sync
    g = lambda k: sh[k]
    PS, attn, gate_a, x1, h2H, h2L = map(g, ("PS", "attn", "gate_a", "x1", "h2H", "h2L"))
    s_xr = sem("s_xr")
    s_xr.inc(act.dma_start(x1[:], t["x"].rearrange("(n p) d -> p n d", p=P)), 16)
    s_x1 = sem("s_x1")
    with ExitStack() as m:
        MH = sb("MH", [P, G, D], F32R, m)
        ML = sb("ML", [P, G, D], F32R, m)
        WO = sb("WO", [P, 2, HG, D], F32, m)
        WV = sb("WV", [P, 2, HG, L], F32, m)
        AH = sb("AH", [P, 2, G, P], F32R, m)
        AL = sb("AL", [P, 2, G, P], F32R, m)
        Y = sb("Y", [P, 2, D], F32, m)
        s_wo = [sem("s_wo0"), sem("s_wo1")]
        s_mm, s_mh, s_ml = sem("s_mm"), sem("s_mh"), sem("s_ml")
        for grp in range(G):
            b = grp % 2
            if grp >= 2:
                wait(sp, s_mm, grp - 1)
            s_wo[b].inc(sp.dma_start(WO[:, b], t["wo"][grp].rearrange("p (h d) -> p h d", h=HG)), 16)
            s_wo[b].inc(sp.dma_start(WV[:, b], t["wv"][grp].rearrange("p (h l) -> p h l", h=HG)), 16)
            wait(pe, s_wo[b], 32 * (grp // 2 + 1))
            for h in range(HG):
                ins = pe.matmul(PS[h * L:(h + 1) * L, grp, :], WV[:, b, h, :], WO[:, b, h, :], start=True, stop=True)
            s_mm.inc(ins)
            wait(act, s_mm, grp + 1)
            s_mh.inc(act.activation(MH[:, grp, :], PS[:, grp, :], ACT.Copy))
            wait(dve, s_mh, grp + 1)
            s_ml.inc(dve.tensor_tensor(ML[:, grp, :], PS[:, grp, :], MH[:, grp, :].bitcast(F32), ALU.subtract))
        s_ah, s_al, s_y, s_yr, s_yg = (sem(n) for n in ("s_ah", "s_al", "s_y", "s_yr", "s_yg"))
        wait(pe, s_ml, G)
        wait(pool, s_xr, 16)
        pe.sem_inc(s_y.h, 2)
        pool.sem_inc(s_yg.h, 2)

        def tile(st, b):
            src = attn[:, :, bass.ds(st * P, P)]
            wait(act, s_y, st + 1)
            s_ah.inc(act.activation(AH[:, b], src, ACT.Copy))
            wait(dve, s_ah, st + 1)
            s_al.inc(dve.tensor_tensor(AL[:, b], src, AH[:, b].bitcast(F32), ALU.subtract))
            wait(pe, s_al, st + 1)
            for n, (a, w) in enumerate(((AH, MH), (AL, MH), (AH, ML))):
                for grp in range(G):
                    ins = pe.matmul(PS[:, b, :], a[:, b, grp, :], w[:, grp, :],
                                    start=(n == 0 and grp == 0), stop=(n == 2 and grp == G - 1))
            s_y.inc(ins)
            wait(dve, s_y, 2 + st + 1)
            wait(dve, s_yg, st + 1)
            s_yr.inc(dve.tensor_tensor(Y[:, b], PS[:, b, :], gate_a[:], ALU.mult))
            wait(pool, s_yr, st + 1)
            dst = x1[:, bass.ds(st, 1), :].rearrange("p n d -> p (n d)")
            s_yg.inc(pool.tensor_tensor(dst, dst, Y[:, b], ALU.add))

        with nc.Fori(0, NS // 2) as i:
            for b in range(2):
                tile(2 * i + b, b)
        for e in (pe, dve, act, sp):
            wait(e, s_yg, 2 + NS)
    nc.all_engine_barrier()
    normalise_transpose(nc, c, sb, sem, wait, "2", x1, lambda e, st: None, lambda e: None, h2H, h2L, dict(sh, which=2))


def phase_ffn(nc, t, c, sb, sem, wait, sh, out):
    pe, act, dve, pool, sp = nc.tensor, nc.scalar, nc.vector, nc.gpsimd, nc.sync
    g = lambda k: sh[k]
    PS, gate_b, x1, h2H, h2L, ffn_s, s_out = map(g, ("PS", "gate_b", "x1", "h2H", "h2L", "ffn_s", "s_out"))
    NCH = NC + 1
    hid = sh["wide"]
    hid_last = sb("hid_last", [P, S], F32, c)
    DH = sb("DH", [P, NCH, D], F32R, c)
    DL = sb("DL", [P, NCH, D], F32R, c)
    with ExitStack() as m:
        WI = sb("WI", [P, 2, 2, KD, P], I32, m)
        WH = sb("FWH", [P, 2, 2, KD, P], F32R, m)
        WL = sb("FWL", [P, 2, 2, KD, P], F32R, m)
        DI = sb("DI", [P, 2, D], I32, m)
        SG = sb("SG", [P, S], F32, m)
        s_w = [sem("s_fw0"), sem("s_fw1")]
        s_h, s_l, s_dl, s_g, s_u, s_sg, s_hid = (sem(n) for n in ("s_fh", "s_fl", "s_fd", "s_fg", "s_fu", "s_sg", "s_hid"))
        for s, n in ((s_l, 2), (s_dl, 2), (s_hid, 2), (s_u, 2)):
            dve.sem_inc(s.h, n)

        def chunk(ch, b, m_=P):
            lo = ch * P
            wait(sp, s_l, ch + 1)
            wait(sp, s_dl, ch + 1)
            turn = (ch - b) // 2 if isinstance(ch, int) else None
            for w, name in ((0, "gate_w"), (1, "up_w")):
                s_w[b].inc(sp.dma_start(WI[:, b, w, :, 0:m_], t[name][:, :, bass.ds(lo, m_)]), 16)
            s_w[b].inc(sp.dma_start(DI[0:m_, b, :], t["down_w"][bass.ds(lo, m_), :]), 16)
            return turn

        def chunk_work(ch, turn, b, m_=P):
            wait(act, s_w[b], 48 * (turn + 1))
            wait(act, s_u, ch + 1)
            s_h.inc(act.activation(WH[:, b, :, :, 0:m_], WI[:, b, :, :, 0:m_], ACT.Copy))
            wait(dve, s_h, 2 * ch + 1)
            s_l.inc(dve.tensor_tensor(WL[:, b, :, :, 0:m_], WI[:, b, :, :, 0:m_], WH[:, b, :, :, 0:m_].bitcast(F32), ALU.subtract))
            dh = DH[0:m_, bass.ds(ch, 1), :].rearrange("p c d -> p (c d)")
            dl = DL[0:m_, bass.ds(ch, 1), :].rearrange("p c d -> p (c d)")
            s_h.inc(act.activation(dh, DI[0:m_, b, :], ACT.Copy))
            wait(dve, s_h, 2 * ch + 2)
            s_dl.inc(dve.tensor_tensor(dl, DI[0:m_, b, :], dh.bitcast(F32), ALU.subtract))
            wait(pe, s_l, 2 + ch + 1)
            wait(pe, s_hid, ch + 1)
            for w, s in ((0, s_g), (1, s_u)):
                for hf in range(2):
                    for n, (a, h) in enumerate(((WH, h2H), (WL, h2H), (WH, h2L))):
                        for k in range(KD):
                            ins = pe.matmul(PS[0:m_, 4 * b + 2 * w + hf, :], a[:, b, w, k, 0:m_],
                                            h[:, k, hf * 512:(hf + 1) * 512],
                                            start=(n == 0 and k == 0), stop=(n == 2 and k == KD - 1))
                s.inc(ins)
            wait(act, s_g, ch + 1)
            wait(act, s_hid, 2 + ch)
            s_sg.inc(act.activation(SG[0:m_, :].rearrange("p (b n) -> p b n", b=2), PS[0:m_, 4 * b:4 * b + 2, :], ACT.Silu,
                                    scale=ffn_s[0:m_, 0:1]))
            wait(dve, s_sg, ch + 1)
            wait(dve, s_u, 2 + ch + 1)
            s_hid.inc(dve.scalar_tensor_tensor(
                out=hid[:, bass.ds(ch, 1), :].rearrange("p c s -> p (c s)") if m_ == P else hid_last[0:m_, :],
                in0=PS[0:m_, 4 * b + 2:4 * b + 4, :].rearrange("p b n -> p (b n)"), scalar=ffn_s[0:m_, 1:2],
                in1=SG[0:m_, :], op0=ALU.mult, op1=ALU.mult))

        with nc.Fori(0, NC // 2) as i:
            for b in range(2):
                chunk(2 * i + b, b)
            for b in range(2):
                chunk_work(2 * i + b, i, b)
        chunk(NC, 0, IT)
        chunk_work(NC, NC // 2, 0, IT)
        wait(act, s_hid, 2 + NCH)
        wait(dve, s_hid, 2 + NCH)
        wait(pe, s_hid, 2 + NCH)
        wait(sp, s_hid, 2 + NCH)
    nc.all_engine_barrier()
    HH = sb("HH", [P, 2, NCH, P], F32R, c)
    HL = sb("HL", [P, 2, NCH, P], F32R, c)
    Y = sb("Y2", [P, 2, D], F32, c)
    OT = sb("OT", [P, 2, D], F32, c)
    s_hh, s_hl, s_y, s_yr, s_ot = (sem(n) for n in ("s_hh", "s_hl", "s_y2", "s_yr2", "s_ot"))
    pe.sem_inc(s_y.h, 2)
    s_st = [sem("s_store0"), sem("s_store1")]
    dve.sem_inc(s_yr.h, 2)
    pool.sem_inc(s_ot.h, 2)
    for s in s_st:
        sp.sem_inc(s.h, 16)

    def tile(st, i, b):
        wait(act, s_y, st + 1)
        for m_, ch in ((P, slice(0, NC)), (IT, slice(NC, NC + 1))):
            src = hid[:, :, bass.ds(st * P, P)] if m_ == P else hid_last[0:m_, bass.ds(st * P, P)]
            dst = HH[0:m_, b, ch, :] if m_ == P else HH[0:m_, b, NC, :]
            dst_lo = HL[0:m_, b, ch, :] if m_ == P else HL[0:m_, b, NC, :]
            s_hh.inc(act.activation(dst, src, ACT.Copy))
            wait(dve, s_hh, 2 * st + (1 if m_ == P else 2))
            s_hl.inc(dve.tensor_tensor(dst_lo, src, dst.bitcast(F32), ALU.subtract))
        wait(pe, s_hl, 2 * st + 2)
        wait(pe, s_yr, st + 1)
        for n, (a, w) in enumerate(((HH, DH), (HL, DH), (HH, DL))):
            for ch in range(NCH):
                k = P if ch < NC else IT
                ins = pe.matmul(PS[:, b, :], a[0:k, b, ch, :], w[0:k, ch, :],
                                start=(n == 0 and ch == 0), stop=(n == 2 and ch == NCH - 1))
        s_y.inc(ins)
        wait(dve, s_y, 2 + st + 1)
        wait(dve, s_ot, st + 1)
        s_yr.inc(dve.scalar_tensor_tensor(out=Y[:, b], in0=PS[:, b, :], scalar=ffn_s[:, 2:3], in1=gate_b[:],
                                          op0=ALU.mult, op1=ALU.mult))
        wait(pool, s_yr, 2 + st + 1)
        wait(pool, s_st[b], 16 * (i + 1))
        s_ot.inc(pool.tensor_tensor(OT[:, b], x1[:, bass.ds(st, 1), :].rearrange("p n d -> p (n d)"), Y[:, b], ALU.add))
        wait(sp, s_ot, 2 + st + 1)
        s_st[b].inc(sp.dma_start(out[bass.ds(st * P, P), :], OT[:, b]), 16)

    with nc.Fori(0, NS // 2) as i:
        for b in range(2):
            tile(2 * i + b, i, b)
    for b in range(2):
        wait(sp, s_st[b], 16 * (NS // 2 + 1))
    nc.all_engine_barrier()


def rotary_tables():
    dim, base, factor, orig = 2 * HALF, 10000.0, 128.0, 1024

    def corr(r):
        return dim * math.log(orig / (r * 2 * math.pi)) / (2 * math.log(base))
    low, high = max(math.floor(corr(32.0)), 0), min(math.ceil(corr(1.0)), dim - 1)
    hi = high + 0.001 if low == high else float(high)
    ramp = np.clip((np.arange(dim // 2, dtype=np.float32) - low) / (hi - low), 0.0, 1.0)
    keep = 1.0 - ramp
    extra = 1.0 / base ** (np.arange(0, dim, 2, dtype=np.float32) / dim)
    inv = extra / factor * (1.0 - keep) + extra * keep
    freqs = np.outer(np.arange(S, dtype=np.float32), inv)
    return np.cos(freqs).astype(np.float32), np.sin(freqs).astype(np.float32)


def kernel(**inputs):
    import concourse.bacc as bacc
    from concourse.bass_utils import run_bass_kernel_spmd

    a = {k: np.asarray(v) for k, v in inputs.items()}
    cosT, sinT = (m.T for m in rotary_tables())
    wq = a["L0_attn_wq_b"].reshape(G, HG, NOPE + 2 * HALF, R)
    pe_rows = wq[:, :, NOPE:, :].reshape(G, HG, HALF, 2, R)
    wkv = a["L0_attn_wkv_b"].reshape(G, HG, NOPE + VD, L)
    ckv, kpe = a["L0_attn_wkv_a"][:L], a["L0_attn_wkv_a"][L:]
    wa = np.concatenate([a["L0_attn_wq_a"], kpe[0::2], kpe[1::2], ckv, kpe[1::2], kpe[0::2]], 0)
    chunks = lambda w: w.T.reshape(KD, P, -1).transpose(1, 0, 2)
    t = {
        "x": a["L0_attn_x"][0],
        "c": a["L0_c"].reshape(KD, P).T,
        "wmod": a["L0_wmod"].reshape(KD, P, 6, D).transpose(2, 1, 0, 3),
        "wa": chunks(wa),
        "lnq": a["L0_attn_q_a_ln_w"].reshape(R, 1),
        "lnkv": a["L0_attn_kv_a_ln_w"].reshape(L, 1),
        "ffn_s": np.tile(np.concatenate([a["L0_ffn_gate_s"], a["L0_ffn_up_s"], a["L0_ffn_down_s"]]), (P, 1)),
        "cos": np.tile(cosT, (4, 1)),
        "sin": np.tile(sinT, (4, 1)),
        "swap_sin": np.concatenate([-sinT, sinT], 0),
        "wq_pe": pe_rows.transpose(0, 4, 3, 1, 2).reshape(G, R, 2 * P),
        "wq_nope": wq[:, :, :NOPE, :].transpose(0, 2, 1, 3).reshape(G, NOPE, HG * R),
        "wk": wkv[:, :, :NOPE, :].transpose(0, 2, 1, 3).reshape(G, NOPE, HG * L),
        "wv": wkv[:, :, NOPE:, :].transpose(0, 2, 1, 3).reshape(G, VD, HG * L),
        "wo": a["L0_attn_wo"].reshape(D, G, HG, VD).transpose(1, 3, 2, 0).reshape(G, VD, HG * D),
        "gate_w": chunks(a["L0_ffn_gate_w"]),
        "up_w": chunks(a["L0_ffn_up_w"]),
        "down_w": a["L0_ffn_down_w"].T,
    }
    nc = bacc.Bacc("TRN2", target_bir_lowering=False, num_devices=1)
    arrays, aps = {}, {}
    for name, v in t.items():
        v = np.ascontiguousarray(v)
        arrays["in_" + name] = v
        aps[name] = nc.dram_tensor("in_" + name, v.shape, mybir.dt.from_np(v.dtype), kind="ExternalInput").ap()
    out = nc.dram_tensor("out_0", (S, D), F32, kind="ExternalOutput").ap()
    build(nc, aps, out)
    r = run_bass_kernel_spmd(nc, [arrays], core_ids=[0])
    return r.results[0]["out_0"].reshape(1, S, D)
```

```python
import concourse.bass as bass
from concourse import mybir
from concourse.alu_op_type import AluOpType as ALU
from contextlib import ExitStack, contextmanager
import math
import numpy as np

F32 = mybir.dt.float32
F32R = mybir.dt.float32r
BF16 = mybir.dt.bfloat16
I32 = mybir.dt.int32
ACT = mybir.ActivationFunctionType
AX = mybir.AxisListType

P = 128
S, D, H = 1024, 512, 32
R, L, HALF = 128, 32, 32
NOPE, VD = 64, 128
I = 1376
G, HG = 8, 4
KR = 2 * HALF + L
KD = D // P
NS = S // P
QB = 512
NQB = S // QB
NC, IT = I // P, I % P
EPS_RMS, EPS_LN = 1e-6, 1e-5
FLOOR = 0.25
MASKED = -1e30
STEPS = [(qb, kt) for qb in range(NQB) for kt in range((qb + 1) * QB // P)]
NSTEP = len(STEPS)
WINDOW_US = 54.0
SLACK = 0.012


def softmax_scale():
    m = 0.1 * math.log(128.0) + 1.0
    return (NOPE + 2 * HALF) ** -0.5 * m * m


def width(qb, kt):
    return min(QB, (qb + 1) * QB - kt * P)


class Count:

    def __init__(self, handle):
        self.h, self.n = handle, 0

    def inc(self, ins, k=1):
        ins.then_inc(self.h, k)
        self.n += k
        return self.n


def build(nc, t, out):
    pe, act, dve, pool, sp = nc.tensor, nc.scalar, nc.vector, nc.gpsimd, nc.sync
    top = ExitStack()
    with top:
        def sem(name):
            return Count(top.enter_context(nc.semaphore(name)))

        def sb(name, shape, dt=F32, where=top):
            return where.enter_context(nc.sbuf_tensor(name, shape, dt))

        s_seen = [sem("s_seen_pool"), sem("s_seen_sp")]

        def wait(eng, s, value):
            eng.wait_ge(s.h, value)
            if not isinstance(value, int) and eng in (sp, pool):
                eng.sem_inc(s_seen[eng is sp].h, 1)

        PS = top.enter_context(nc.psum_tensor("PS", [P, 8, 512], F32))
        ident = sb("ident", [P, P])
        ones = sb("ones", [P, P])
        gate_a = sb("gate_a", [P, D])
        gate_b = sb("gate_b", [P, D])
        lnq = sb("lnq", [P, 1])
        lnkv = sb("lnkv", [P, 1])
        ffn_s = sb("ffn_s", [P, 3])
        mod_col = sb("mod_col", [P, 4, KD])
        eps = sb("eps", [P, 2])
        stats = sb("stats", [P, NS, 6])
        mv = sb("mv", [P, NS, 2])
        rstd = sb("rstd", [P, NS])
        wide = sb("wide", [P, NC, S])
        attn = wide[:, 0:G, :]

        s_const, s_small, s_x = sem("s_const"), sem("s_small"), sem("s_x")
        s_out = sem("s_out")

        def barrier():
            nc.all_engine_barrier()

        s_const.inc(pool.memset(ident[:], 0.0))
        s_const.inc(pool.memset(ones[:], 1.0))
        s_const.inc(pool.memset(eps[:, 0:1], EPS_RMS))
        s_const.inc(pool.memset(eps[:, 1:2], EPS_LN))
        wait(pool, s_const, 4)
        s_const.inc(pool.affine_select(out=ident[:], in_=ident[:], compare_op=ALU.not_equal, fill=1.0,
                                       base=0, pattern=[[-1, P]], channel_multiplier=1))

        with ExitStack() as shared:
            KH = sb("KH", [P, S], F32R, shared)
            KL = sb("KL", [P, S], F32R, shared)
            V = sb("V", [P, NS, L], F32, shared)
            QNH = sb("QNH", [P, S], F32R, shared)
            QNL = sb("QNL", [P, S], F32R, shared)
            cos = sb("cos", [P, S], F32, shared)
            sin = sb("sin", [P, S], F32, shared)

            with ExitStack() as c:
                phase_inputs(nc, t, c, sb, sem, wait, locals())
            barrier()
            with ExitStack() as c:
                phase_attention(nc, t, c, sb, sem, wait, locals())
            barrier()
        x1 = sb("x1", [P, NS, D])
        h2H = sb("h2H", [P, KD, S], F32R)
        h2L = sb("h2L", [P, KD, S], F32R)
        with ExitStack() as c:
            phase_project(nc, t, c, sb, sem, wait, locals())
        barrier()
        with ExitStack() as c:
            phase_ffn(nc, t, c, sb, sem, wait, locals(), out)


def normalise_transpose(nc, c, sb, sem, wait, tag, x, ready, mod, outH, outL, sh):
    pe, act, dve, pool = nc.tensor, nc.scalar, nc.vector, nc.gpsimd
    PS, ident, mv, stats, rstd, mod_col, eps = (sh[k] for k in ("PS", "ident", "mv", "stats", "rstd", "mod_col", "eps"))
    xn = sb("xn" + tag, [P, NS, D], F32, c)
    full = sb("hfull" + tag, [P, 2, 512], F32, c)
    s_mv, s_sq, s_rs, s_xn, s_tr, s_full, s_hi, s_lo = (sem(n + tag) for n in (
        "s_mv", "s_sq", "s_rs", "s_xn", "s_tr", "s_full", "s_hi", "s_lo"))
    for st in range(NS):
        ready(dve, st)
        s_mv.inc(dve.bn_stats(stats[:, st, :], x[:, st, :]))
        wait(dve, s_mv, s_mv.n)
        s_mv.inc(dve.bn_aggr(mv[:, st, :], stats[:, st, :]))
        if st % 4 == 3:
            half = slice(st - 3, st + 1)
            wait(act, s_mv, s_mv.n)
            s_sq.inc(act.activation(rstd[:, half], mv[:, half, 1], ACT.Sqrt, bias=eps[:, 1:2]))
            wait(dve, s_sq, s_sq.n)
            s_rs.inc(dve.reciprocal(rstd[:, half], rstd[:, half]))
            wait(dve, s_rs, s_rs.n)
            for k in range(st - 3, st + 1):
                s_xn.inc(dve.tensor_scalar(xn[:, k, :], x[:, k, :], mv[:, k, 0:1], rstd[:, k:k + 1],
                                           ALU.subtract, ALU.mult))
    for n in range(2 * KD):
        hf, d = divmod(n, KD)
        wait(pe, s_xn, 4 * (hf + 1))
        for k in range(4):
            ins = pe.transpose(PS[:, n, k * P:(k + 1) * P], xn[:, 4 * hf + k, d * P:(d + 1) * P], ident[:])
        s_tr.inc(ins)
        cols = slice(hf * 512, hf * 512 + 512)
        wait(act, s_tr, s_tr.n)
        mod(act)
        if n >= 2:
            wait(act, s_lo, n - 1)
        s_full.inc(act.activation(full[:, n % 2, :], PS[:, n, :], ACT.Identity,
                                  scale=mod_col[:, sh["which"], d:d + 1], bias=mod_col[:, sh["which"] + 1, d:d + 1]))
        wait(dve, s_full, n + 1)
        s_hi.inc(dve.tensor_copy(outH[:, d, cols], full[:, n % 2, :]))
        wait(pool, s_hi, n + 1)
        s_lo.inc(pool.tensor_tensor(outL[:, d, cols], full[:, n % 2, :], outH[:, d, cols].bitcast(F32), ALU.subtract))
    return s_hi, s_lo, s_tr, s_full


def phase_inputs(nc, t, c, sb, sem, wait, sh):
    pe, act, dve, pool, sp = nc.tensor, nc.scalar, nc.vector, nc.gpsimd, nc.sync
    g = lambda k: sh[k]
    PS, ident, ones, KH, KL, V, QNH, QNL, cos, sin = map(g, ("PS", "ident", "ones", "KH", "KL", "V", "QNH", "QNL", "cos", "sin"))
    gate_a, gate_b, lnq, lnkv, ffn_s, mod_col, eps = map(g, (
        "gate_a", "gate_b", "lnq", "lnkv", "ffn_s", "mod_col", "eps"))
    s_const, s_small = g("s_const"), g("s_small")
    x = sb("x_in", [P, NS, D], F32, c)
    cT = sb("cT", [P, 3, KD], F32, c)
    wm = sb("wm", [P, 2, KD, D], F32, c)
    WA = sb("WA", [P, KD, R + KR + 2 * HALF], F32, c)
    WAH = sb("WAH", [P, KD, R + KR + 2 * HALF], F32R, c)
    WAL = sb("WAL", [P, KD, R + KR + 2 * HALF], F32R, c)
    hH = sb("hH", [P, KD, S], F32R, c)
    hL = sb("hL", [P, KD, S], F32R, c)
    tmp = sb("tmp", [P, 3, 512], F32, c)
    swap_sin = sb("swap_sin", [2 * HALF, S], F32, c)
    KF = sb("KF", [P, S], F32, c)
    scb = sb("scb", [P, KD, P], F32, c)

    s_xt = [sem(f"s_xt{i}") for i in range(NS)]
    s_wm = [sem(f"s_wm{i}") for i in range(6)]
    s_wa, s_rope = sem("s_wa"), sem("s_rope")
    s_small.inc(sp.dma_start(cT[:, 0, :], t["c"]), 16)
    xt = t["x"].rearrange("(n p) d -> p n d", p=P)
    for st in range(NS):
        s_xt[st].inc(act.dma_start(x[:, st, :], xt[:, st, :]), 16)
    for b, k in enumerate((1, 0)):
        s_wm[b].inc(sp.dma_start(wm[:, b, :, :], t["wmod"][k]), 16)
    s_wa.inc(sp.dma_start(WA[:], t["wa"]), 16)
    s_small.inc(sp.dma_start(lnq[:], t["lnq"]), 16)
    s_small.inc(sp.dma_start(lnkv[2 * HALF:KR, :], t["lnkv"]), 16)
    s_small.inc(sp.dma_start(ffn_s[:], t["ffn_s"]), 16)
    s_rope.inc(sp.dma_start(cos[:], t["cos"]), 16)
    s_rope.inc(sp.dma_start(sin[:], t["sin"]), 16)
    s_rope.inc(sp.dma_start(swap_sin[:], t["swap_sin"]), 16)

    s_c = sem("s_c")
    wait(act, s_small, 64)
    s_c.inc(act.activation(cT[:, 1, :], cT[:, 0, :], ACT.Silu))
    wait(dve, s_small, 64)
    wait(dve, s_const, 5)
    dve.tensor_scalar(lnq[:], lnq[:], softmax_scale(), None, ALU.mult)
    wait(dve, s_c, 1)
    for k in range(KD):
        last = dve.tensor_scalar(scb[:, k, :], ones[:], cT[:, 1, k:k + 1], None, ALU.mult)
    s_scb = sem("s_scb")
    s_scb.inc(last)

    s_m, s_mc = sem("s_m"), sem("s_mc")
    ORDER = [1, 0, 4, 3, 2, 5]
    wait(pe, s_const, 5)
    wait(pe, s_scb, 1)
    for n, which in enumerate(ORDER):
        b = n % 2
        if n >= 2:
            wait(sp, s_m, n - 1)
            s_wm[n].inc(sp.dma_start(wm[:, b, :, :], t["wmod"][which]), 16)
        wait(pe, s_wm[n], 16)
        if n < 4:
            for d in range(KD):
                for k in range(KD):
                    ins = pe.matmul(PS[:, 7, 8 * n + d:8 * n + d + 1], wm[:, b, k, d * P:(d + 1) * P], cT[:, 1, k:k + 1],
                                    start=(k == 0), stop=(k == KD - 1))
            s_m.inc(ins)
            wait(dve, s_m, n + 1)
            dst = mod_col[:, n, :]
            src = PS[:, 7, 8 * n:8 * n + KD]
            s_mc.inc(dve.tensor_scalar(dst, src, 1.0 if n % 2 == 0 else 0.0, None, ALU.add))
            wait(pe, s_mc, n + 1)
        else:
            for k in range(KD):
                ins = pe.matmul(PS[:, n, :], scb[:, k, :], wm[:, b, k, :], start=(k == 0), stop=(k == KD - 1))
            s_m.inc(ins)
            wait(dve, s_m, n + 1)
            s_mc.inc(dve.tensor_copy(tmp[:, 0, :], PS[:, n, :]))
            wait(dve, s_mc, s_mc.n)
            dst = gate_a if n == 4 else gate_b
            s_mc.inc(dve.tensor_scalar(tmp[:, 1, :], tmp[:, 0, :], -1.0, None, ALU.mult))
            wait(dve, s_mc, s_mc.n)
            s_mc.inc(dve.tensor_tensor(tmp[:, 1, :], tmp[:, 0, :], tmp[:, 1, :], ALU.max))
            wait(dve, s_mc, s_mc.n)
            s_mc.inc(dve.tensor_scalar(tmp[:, 1, :], tmp[:, 1, :], FLOOR, None, ALU.max))
            s_mc.inc(dve.tensor_scalar(tmp[:, 0, :], tmp[:, 0, :], 0.0, 2.0, ALU.is_ge, ALU.mult))
            wait(dve, s_mc, s_mc.n)
            s_mc.inc(dve.scalar_tensor_tensor(out=dst[:], in0=tmp[:, 0, :], scalar=-1.0, in1=tmp[:, 1, :],
                                              op0=ALU.add, op1=ALU.mult))
            wait(pe, s_mc, s_mc.n)
            wait(dve, s_mc, s_mc.n)

    s_wah = sem("s_wah")
    wait(act, s_wa, 16)
    s_wah.inc(act.activation(WAH[:], WA[:], ACT.Copy))
    wait(pool, s_wah, 1)
    s_wal = sem("s_wal")
    s_wal.inc(pool.tensor_tensor(WAL[:], WA[:], WAH[:].bitcast(F32), ALU.subtract))

    s_hi, s_lo, s_tr, s_full = normalise_transpose(
        nc, c, sb, sem, wait, "1", x, lambda e, st: wait(e, s_xt[st], 16), lambda e: wait(e, s_mc, 4), hH, hL,
        dict(sh, which=0))

    s_pj, s_sq, s_ss, s_rt, s_inv, s_kv = (sem(n) for n in ("s_pj", "s_sqr", "s_ss", "s_rt", "s_inv", "s_kv"))
    s_ev = sem("s_ev")
    wait(pe, s_wal, 1)
    wait(pe, s_full, 2 * KD)
    for hf in range(2):
        cols = slice(hf * 512, hf * 512 + 512)
        wait(pe, s_lo, KD * (hf + 1))
        for bank, lo, m in ((hf, 0, R), (2 + hf, R, KR), (4 + hf, R + KR, 2 * HALF)):
            for n, (w, h) in enumerate(((WAH, hH), (WAL, hH), (WAH, hL))):
                for k in range(KD):
                    ins = pe.matmul(PS[0:m, bank, :], w[:, k, lo:lo + m], h[:, k, cols],
                                    start=(n == 0 and k == 0), stop=(n == 2 and k == KD - 1))
            s_pj.inc(ins)
    lat = slice(2 * HALF, KR)
    rot = slice(0, 2 * HALF)
    wait(dve, s_rope, 48)
    for hf in range(2):
        cols = slice(hf * 512, hf * 512 + 512)
        wait(act, s_pj, 3 * hf + 1)
        if hf:
            wait(act, s_kv, 1)
        s_sq.inc(act.activation(tmp[:, 0, :], PS[:, hf, :], ACT.Square))
        wait(act, s_pj, 3 * hf + 2)
        s_sq.inc(act.activation(tmp[lat, 1, :], PS[lat, 2 + hf, :], ACT.Square))
        wait(pe, s_sq, 2 * hf + 1)
        if hf:
            wait(pe, s_rt, 2)
        s_ss.inc(pe.matmul(PS[:, 6, :], ones[:], tmp[:, 0, :], start=True, stop=True))
        wait(pe, s_sq, 2 * hf + 2)
        s_ss.inc(pe.matmul(PS[lat, 7, :], ones[lat, 0:L], tmp[lat, 1, :], start=True, stop=True))
        wait(act, s_ss, 2 * hf + 1)
        s_rt.inc(act.activation(tmp[:, 0, :], PS[:, 6, :], ACT.Sqrt, scale=1.0 / R, bias=eps[:, 0:1]))
        wait(act, s_ss, 2 * hf + 2)
        s_rt.inc(act.activation(tmp[lat, 1, :], PS[lat, 7, :], ACT.Sqrt, scale=1.0 / L, bias=eps[lat, 0:1]))
        wait(dve, s_rt, 2 * hf + 1)
        s_inv.inc(dve.reciprocal(tmp[:, 0, :], tmp[:, 0, :]))
        wait(dve, s_rt, 2 * hf + 2)
        s_inv.inc(dve.reciprocal(tmp[lat, 1, :], tmp[lat, 1, :]))
        wait(dve, s_inv, 2 * hf + 2)
        if hf:
            wait(dve, s_kv, 2)
        s_ev.inc(dve.tensor_tensor(tmp[:, 2, :], PS[:, hf, :], tmp[:, 0, :], ALU.mult))
        wait(dve, s_ev, s_ev.n)
        s_ev.inc(dve.tensor_copy(QNH[:, cols], tmp[:, 2, :]))
        wait(dve, s_ev, s_ev.n)
        s_ev.inc(dve.tensor_tensor(QNL[:, cols], tmp[:, 2, :], QNH[:, cols].bitcast(F32), ALU.subtract))
        s_ev.inc(dve.scalar_tensor_tensor(out=KF[lat, cols], in0=PS[lat, 2 + hf, :], scalar=lnkv[lat, :],
                                          in1=tmp[lat, 1, :], op0=ALU.mult, op1=ALU.mult))
        wait(dve, s_ev, s_ev.n)
        s_ev.inc(dve.tensor_tensor(tmp[rot, 2, :], PS[rot, 2 + hf, :], cos[rot, cols], ALU.mult))
        wait(dve, s_pj, 3 * hf + 3)
        s_ev.inc(dve.tensor_tensor(tmp[rot, 0, :], PS[rot, 4 + hf, :], swap_sin[:, cols], ALU.mult))
        wait(dve, s_ev, s_ev.n)
        s_kv.inc(dve.tensor_tensor(KF[rot, cols], tmp[rot, 2, :], tmp[rot, 0, :], ALU.add))
        wait(dve, s_kv, s_kv.n)
        s_kv.inc(dve.tensor_copy(KH[0:KR, cols], KF[0:KR, cols]))
        wait(dve, s_kv, s_kv.n)
        s_kv.inc(dve.tensor_tensor(KL[0:KR, cols], KF[0:KR, cols], KH[0:KR, cols].bitcast(F32), ALU.subtract))
    s_k1 = sem("s_k1")
    s_k1.inc(dve.memset(KH[KR:, :].bitcast(F32), 0.0))
    s_k1.inc(dve.memset(KL[KR:, :].bitcast(F32), 0.0))
    wait(dve, s_k1, 2)
    s_k1.inc(dve.memset(KH[KR:KR + 1, :].bitcast(F32), 1.0))
    wait(pe, s_kv, 6)
    wait(pe, s_inv, 4)
    wait(pe, s_rt, 4)
    for kt in range(NS):
        ins = pe.transpose(PS[:, 6, kt * L:(kt + 1) * L], KF[lat, kt * P:(kt + 1) * P], ident[lat, lat])
    s_v = sem("s_v")
    s_v.inc(ins)
    wait(dve, s_v, 1)
    s_k1.inc(dve.tensor_copy(V[:].rearrange("p n l -> p (n l)"), PS[:, 6, 0:NS * L]))
    wait(dve, s_k1, 4)


def phase_attention(nc, t, c, sb, sem, wait, sh):
    pe, act, dve, pool, sp = nc.tensor, nc.scalar, nc.vector, nc.gpsimd, nc.sync
    g = lambda k: sh[k]
    PS, ident, ones, KH, KL, V, QNH, QNL, cos, sin = map(g, ("PS", "ident", "ones", "KH", "KL", "V", "QNH", "QNL", "cos", "sin"))
    lnq, attn = g("lnq"), g("attn")
    Q = sb("Q", [P, 2, 2, HG, S], F32R, c)
    WP = sb("WP", [P, 2 * P], F32, c)
    WN = sb("WN", [NOPE, HG, R], F32, c)
    WK = sb("WK", [NOPE, HG, L], F32, c)
    WF = sb("WF", [P, 3 * P], F32, c)
    WH = sb("WH", [P, 3 * P], F32R, c)
    WL = sb("WL", [P, 3 * P], F32R, c)
    RT = sb("RT", [P, 4, 512], F32, c)
    RE = sb("RE", [P, 2, 512], F32, c)
    TQ = sb("TQ", [P, 3, 2, S], F32R, c)
    PR = sb("PR", [P, 3, HG, QB], F32, c)
    NMa = sb("NMa", [P, HG, NS], F32, c)
    NMb = sb("NMb", [P, HG, NS // 2], F32, c)
    NM = sb("NM", [HG * NS, P], F32R, c)
    RD = sb("RD", [P, QB], F32, c)
    identb = sb("identb", [P, P], BF16, c)
    maskb = sb("maskb", [P, P], BF16, c)

    s_w = sem("s_w")
    s_wf = sem("s_wf")
    s_wh = sem("s_wh")
    s_wl = sem("s_wl")
    s_af = sem("s_af")
    s_ar = sem("s_ar")
    s_re = sem("s_re")
    s_th = sem("s_th")
    s_lh = sem("s_lh")
    s_tl = sem("s_tl")
    s_q = [sem(f"s_q{h}") for h in range(HG)]
    s_nm = sem("s_nm")
    s_nd = sem("s_nd")
    s_st = sem("s_st")
    s_p = sem("s_p")
    s_pv = sem("s_pv")
    s_o = sem("s_o")
    s_rd = sem("s_rd")
    s_no = sem("s_no")
    s_mk = sem("s_mk")
    UQ = 1 + 3 * NQB
    UM = HG * (NS + NS // 2) + 1
    UNITS = UQ + UM
    unit_of = {}
    NPAIR = 2 * NSTEP

    for par in range(2):
        for hl in range(2):
            s_mk.inc(dve.memset(Q[KR:, par, hl].bitcast(F32), 0.0))
    s_mk.inc(pool.memset(identb[:], 0.0))
    s_mk.inc(pool.memset(maskb[:], 0.0))
    wait(pool, s_mk, 6)
    s_mk.inc(pool.affine_select(out=identb[:], in_=identb[:], compare_op=ALU.not_equal, fill=1.0, base=0,
                                pattern=[[-1, P]], channel_multiplier=1))
    s_mk.inc(pool.affine_select(out=maskb[:], in_=maskb[:], compare_op=ALU.is_ge, fill=MASKED, base=0,
                                pattern=[[-1, P]], channel_multiplier=1))
    wait(pe, s_mk, 8)
    wait(sp, s_mk, 8)
    dve.sem_inc(s_ar.h, 2)
    act.sem_inc(s_o.h, 2)
    pool.sem_inc(s_no.h, 1)
    pool.sem_inc(s_wl.h, 1)
    pool.sem_inc(s_re.h, 1)
    pool.sem_inc(s_tl.h, 1)
    sp.sem_inc(s_nd.h, 16)
    for h in range(HG):
        sp.sem_inc(s_q[h].h, 48)
    act.sem_inc(s_p.h, 2)
    pe.sem_inc(s_pv.h, 3)
    pe.sem_inc(s_st.h, NPAIR)

    def load_weights(grp):
        s_w.inc(sp.dma_start(WP[:], t["wq_pe"][bass.ds(grp, 1)].rearrange("g p n -> (g p) n")), 16)
        s_w.inc(sp.dma_start(WN[:].rearrange("p h r -> p (h r)"),
                             t["wq_nope"][bass.ds(grp, 1)].rearrange("g p n -> (g p) n")), 16)
        s_w.inc(sp.dma_start(WK[:].rearrange("p h r -> p (h r)"),
                             t["wk"][bass.ds(grp, 1)].rearrange("g p n -> (g p) n")), 16)

    def send_queries(grp, par):
        wait(sp, s_tl, 1 + 2 * (grp + 1))
        if not isinstance(grp, int) or grp > 1:
            wait(sp, s_st, NPAIR + NPAIR * (grp - 1))
        for h in range(HG):
            for b in range(3):
                s_q[h].inc(sp.dma_start(Q[b * 32:(b + 1) * 32, par, :, h, :].bitcast(F32),
                                        TQ[h * 32:(h + 1) * 32, b, :, :].bitcast(F32)), 16)

    class Side:

        def __init__(self, first, parity):
            self.first, self.parity, self.at = first, parity, 0

        def take(self):
            n, u = self.first + self.at, (self.parity + self.at) % 2
            self.at += 1
            wait(pe, s_ar, n + 1)
            return n, PS[:, 6 + u, :]

    def queries(side, grp):

        def weights():
            n, bank = side.take()
            unit_of["weights"] = side.at
            wait(pe, s_w, 48 * (grp + 1))
            for h in range(HG):
                ins = pe.matmul(bank[:, h * L:(h + 1) * L], WN[:, h, :], WK[:, h, :], start=True, stop=True)
            s_af.inc(ins)
            wait(dve, s_w, 48 * (grp + 1))
            wait(dve, s_wl, 1 + grp)
            s_wf.inc(dve.tensor_scalar(WF[:, 0:2 * P], WP[:], lnq[:], None, ALU.mult))
            wait(dve, s_af, n + 1)
            s_ar.inc(dve.tensor_scalar(WF[:, 2 * P:], bank[:, 0:HG * L], lnq[:], None, ALU.mult))
            wait(act, s_wf, grp + 1)
            wait(act, s_ar, 2 + n + 1)
            s_wh.inc(act.activation(WH[:], WF[:], ACT.Copy))
            wait(pool, s_wh, grp + 1)
            s_wl.inc(pool.tensor_tensor(WL[:], WF[:], WH[:].bitcast(F32), ALU.subtract))

        def project(block, hf):
            cols = slice(hf * 512, hf * 512 + 512)
            n, bank = side.take()
            wait(pe, s_wl, 1 + grp + 1)
            for k, (w, q) in enumerate(((WH, QNH), (WL, QNH), (WH, QNL))):
                ins = pe.matmul(bank, w[:, block * P:(block + 1) * P], q[:, cols], start=(k == 0), stop=(k == 2))
            s_af.inc(ins)
            return n, bank

        def even(hf):
            cols = slice(hf * 512, hf * 512 + 512)
            n, bank = project(0, hf)
            wait(dve, s_af, n + 1)
            wait(dve, s_re, 2 * (2 * grp + hf) + 1)
            dve.tensor_tensor(RT[:, 0, :], bank, cos[:, cols], ALU.mult)
            s_ar.inc(dve.tensor_tensor(RT[:, 3, :], bank, sin[:, cols], ALU.mult))

        def odd(hf):
            cols = slice(hf * 512, hf * 512 + 512)
            half = 2 * grp + hf
            n, bank = project(1, hf)
            wait(dve, s_af, n + 1)
            dve.tensor_tensor(RT[:, 1, :], bank, sin[:, cols], ALU.mult)
            s_ar.inc(dve.tensor_tensor(RT[:, 2, :], bank, cos[:, cols], ALU.mult))
            wait(pool, s_ar, 2 + n + 1)
            wait(pool, s_tl, half + 1)
            s_re.inc(pool.tensor_tensor(RE[:, 0, :], RT[:, 0, :], RT[:, 1, :], ALU.subtract))
            s_re.inc(pool.tensor_tensor(RE[:, 1, :], RT[:, 2, :], RT[:, 3, :], ALU.add))

        def latent(hf):
            cols = slice(hf * 512, hf * 512 + 512)
            n, bank = project(2, hf)
            if hf == 0:
                for h in range(HG):
                    wait(dve, s_q[h], 48 * (grp + 1))
            wait(dve, s_af, n + 1)
            s_lh.inc(dve.tensor_copy(TQ[:, 2, 0, cols], bank))
            wait(dve, s_lh, 2 * grp + hf + 1)
            s_ar.inc(dve.tensor_tensor(TQ[:, 2, 1, cols], bank, TQ[:, 2, 0, cols].bitcast(F32), ALU.subtract))
            wait(pool, s_ar, 2 + n + 1)

        def split(hf):
            cols = slice(hf * 512, hf * 512 + 512)
            half = 2 * grp + hf
            if hf == 0:
                for h in range(HG):
                    wait(act, s_q[h], 48 * (grp + 1))
            wait(act, s_re, 1 + 2 * half + 2)
            s_th.inc(act.activation(TQ[:, 0:2, 0, cols], RE[:], ACT.Copy))
            wait(pool, s_th, half + 1)
            s_tl.inc(pool.tensor_tensor(TQ[:, 0:2, 1, cols], RE[:], TQ[:, 0:2, 0, cols].bitcast(F32), ALU.subtract))

        return [(0.15, weights, 0.7), (0.25, lambda: even(0), 1.2), (0.28, lambda: odd(0), 1.2),
                (0.36, lambda: latent(0), 1.3), (0.40, lambda: split(0), 0.0), (0.54, lambda: even(1), 1.2),
                (0.57, lambda: odd(1), 1.2), (0.65, lambda: latent(1), 1.3), (0.70, lambda: split(1), 0.0)]

    def maxima(side, grp, par):

        def part_of(h, qt, part):
            n, bank = side.take()
            wait(pe, s_q[h], 48 * (grp + 2))
            lo = part * 512
            w = min(512, (qt + 1) * P - lo)
            diagonal = (qt + 1) * P == lo + w
            ins = pe.matmul(bank[:, 0:w], Q[0:KR, par, 0, h, qt * P:(qt + 1) * P], KH[0:KR, lo:lo + w],
                            start=True, stop=not diagonal)
            if diagonal:
                ins = pe.matmul(bank[:, w - P:w], identb[:], maskb[:], start=False, stop=True)
            s_af.inc(ins)
            wait(dve, s_af, n + 1)
            dst = NMb[:, h, qt - NS // 2:qt - NS // 2 + 1] if part else NMa[:, h, qt:qt + 1]
            s_ar.inc(dve.tensor_reduce(dst, bank[:, 0:w], axis=AX.X, op=ALU.max, negate=True))

        def combine():
            wait(dve, s_ar, 2 + side.first + side.at)
            s_nm.inc(dve.tensor_tensor(NMa[:, :, NS // 2:], NMa[:, :, NS // 2:], NMb[:], ALU.min))

        def rows():
            n, bank = side.take()
            wait(pe, s_nm, grp + 1)
            s_af.inc(pe.transpose(bank[0:HG * NS, 0:P], NMa[:].rearrange("p h n -> p (h n)"), ident[:]))
            wait(dve, s_af, n + 1)
            wait(dve, s_nd, 16 * (grp + 1))
            s_ar.inc(dve.tensor_copy(NM[:], bank[0:HG * NS, 0:P]))
            wait(sp, s_ar, 2 + n + 1)
            s_nd.inc(sp.dma_start(Q[KR:KR + 1, par, 0, :, :].rearrange("p h (n q) -> p (h n) q", q=P).bitcast(F32),
                                  NM[:].bitcast(F32)), 16)

        parts = [(h, qt, part) for h in range(HG) for qt in range(NS) for part in range(1 + qt * P // 512)]
        cost = [0.12 + min(512, (qt + 1) * P - part * 512) / 960 for _, qt, part in parts]
        begin, end = 0.08, 0.82
        work = []
        for k, (h, qt, part) in enumerate(parts):
            work.append((begin + (end - begin) * sum(cost[:k]) / sum(cost),
                         lambda h=h, qt=qt, part=part: part_of(h, qt, part), cost[k]))
        return work + [(end + 0.01, combine, 0.1), (end + 0.02, rows, 0.3)]

    def scores(grp, par, s, h):
        qb, kt = STEPS[s]
        w = width(qb, kt)
        q0 = (qb + 1) * QB - w
        diagonal = kt * P >= qb * QB
        p = h // 2
        pair = NPAIR * grp + 2 * s + p
        if h % 2 == 0:
            wait(pe, s_p, pair + 1)
        if s == 0 and h == 0:
            wait(pe, s_nd, 16 * (grp + 2))
        ks = slice(kt * P, (kt + 1) * P)
        dst = PS[:, h, 0:w]
        pe.matmul(dst, KH[:, ks], Q[:, par, 0, h, q0:q0 + w], start=True, stop=False)
        pe.matmul(dst, KL[:, ks], Q[:, par, 0, h, q0:q0 + w], start=False, stop=False)
        ins = pe.matmul(dst, KH[:, ks], Q[:, par, 1, h, q0:q0 + w], start=False, stop=not diagonal)
        if diagonal:
            ins = pe.matmul(PS[:, h, 0:P], maskb[:], identb[:], start=False, stop=True)
        if h % 2:
            s_st.inc(ins)
            wait(act, s_st, NPAIR + pair + 1)
            wait(act, s_pv, NSTEP * grp + s + 1)
            s_p.inc(act.activation(PR[:, s % 3, 2 * p:2 * p + 2, 0:w], PS[:, 2 * p:2 * p + 2, 0:w], ACT.Exp))

    def values(grp, s, bank):
        qb, kt = STEPS[s]
        w = width(qb, kt)
        if bank == 4:
            wait(pe, s_p, 2 + NPAIR * grp + 2 * s + 2)
            if kt == 0:
                wait(pe, s_o, 2 + 2 * (2 * grp + qb))
        for h in range(HG):
            ins = pe.matmul(PS[h * L:(h + 1) * L, bank, QB - w:QB], V[:, kt, :] if bank == 4 else ones[:, 0:L],
                            PR[:, s % 3, h, 0:w], start=(kt == 0), stop=(kt == (qb + 1) * QB // P - 1))
        if bank == 5:
            s_pv.inc(ins)

    def empty(grp, qb):
        wait(act, s_pv, 3 + NSTEP * grp + (4 if qb == 0 else NSTEP))
        wait(act, s_no, 1 + 2 * grp + qb)
        s_o.inc(act.activation(RD[:], PS[:, 5, :], ACT.Copy))
        s_o.inc(act.activation(out_of(grp, qb), PS[:, 4, :], ACT.Copy))

    def out_of(grp, qb):
        return attn[:, bass.ds(grp, 1), qb * QB:(qb + 1) * QB].rearrange("p g q -> p (g q)")

    def invert(grp, qb, n):
        wait(dve, s_o, 2 + 2 * (2 * grp + qb) + 1)
        ap = RD[:, n * P:(n + 1) * P]
        s_rd.inc(dve.reciprocal(ap, ap))

    def normalise(grp, qb):
        wait(pool, s_o, 2 + 2 * (2 * grp + qb) + 2)
        wait(pool, s_rd, 4 * (2 * grp + qb + 1))
        s_no.inc(pool.tensor_tensor(out_of(grp, qb), out_of(grp, qb), RD[:], ALU.mult))

    def window(grp, par, with_maxima, with_queries):
        side = Side(UQ + UNITS * (grp + 1), UQ % 2)
        work = []
        if with_queries:
            wait(sp, s_wf, grp + 2)
            wait(sp, s_af, UQ + UNITS * grp + unit_of["weights"])
            load_weights(grp + 2)
        if with_maxima:
            send_queries(grp + 1, 1 - par)
            work += maxima(side, grp + 1, 1 - par)
        if with_queries:
            work += queries(side, grp + 2)
        total = sum(width(*STEPS[s]) for s in range(NSTEP))
        place = free = 0.0

        def advance(cost, everything=False):
            nonlocal place, free
            place += cost / total
            work.sort(key=lambda x: x[0])
            while work and (everything or max(work[0][0], free - SLACK) <= place):
                _, f, busy = work.pop(0)
                f()
                free = max(free, place) + busy / WINDOW_US

        for s in range(NSTEP + 1):
            if s < NSTEP:
                for h in range(HG):
                    scores(grp, par, s, h)
                    advance(3 * width(*STEPS[s]) / 16)
            if s > 0:
                if s == NSTEP:
                    advance(0, everything=True)
                for bank in (4, 5):
                    values(grp, s - 1, bank)
                    advance(width(*STEPS[s - 1]) / 8)
            if s == 4:
                empty(grp, 0)
                work += [(place + 0.03 * n, lambda n=n: invert(grp, 0, n), 0.9) for n in range(4)]
                work.append((place + 0.1, lambda: normalise(grp, 0), 0.0))
        empty(grp, 1)
        for n in range(4):
            invert(grp, 1, n)
        normalise(grp, 1)

    load_weights(0)
    first = Side(0, 0)
    for _, f, _ in queries(first, 0):
        f()
    send_queries(0, 0)
    ahead = Side(UQ, UQ % 2)
    wait(sp, s_wf, 1)
    load_weights(1)
    work = maxima(ahead, 0, 0) + queries(ahead, 1)
    for _, f, _ in sorted(work, key=lambda x: x[0]):
        f()
    with nc.Fori(0, (G - 2) // 2) as i:
        window(2 * i, 0, True, True)
        window(2 * i + 1, 1, True, True)
    window(G - 2, 0, True, False)
    window(G - 1, 1, False, False)
    for e in (act, pe, dve):
        wait(e, s_no, 1 + 2 * G)
    wait(sp, s_nd, 16 * (G + 1))


def phase_project(nc, t, c, sb, sem, wait, sh):
    pe, act, dve, pool, sp = nc.tensor, nc.scalar, nc.vector, nc.gpsimd, nc.sync
    g = lambda k: sh[k]
    PS, attn, gate_a, x1, h2H, h2L = map(g, ("PS", "attn", "gate_a", "x1", "h2H", "h2L"))
    s_xr = sem("s_xr")
    s_xr.inc(act.dma_start(x1[:], t["x"].rearrange("(n p) d -> p n d", p=P)), 16)
    s_x1 = sem("s_x1")
    with ExitStack() as m:
        MH = sb("MH", [P, G, D], F32R, m)
        ML = sb("ML", [P, G, D], F32R, m)
        WO = sb("WO", [P, 2, HG, D], F32, m)
        WV = sb("WV", [P, 2, HG, L], F32, m)
        AH = sb("AH", [P, 2, G, P], F32R, m)
        AL = sb("AL", [P, 2, G, P], F32R, m)
        Y = sb("Y", [P, 2, D], F32, m)
        s_wo = [sem("s_wo0"), sem("s_wo1")]
        s_mm, s_mh, s_ml = sem("s_mm"), sem("s_mh"), sem("s_ml")
        for grp in range(G):
            b = grp % 2
            if grp >= 2:
                wait(sp, s_mm, grp - 1)
            s_wo[b].inc(sp.dma_start(WO[:, b], t["wo"][grp].rearrange("p (h d) -> p h d", h=HG)), 16)
            s_wo[b].inc(sp.dma_start(WV[:, b], t["wv"][grp].rearrange("p (h l) -> p h l", h=HG)), 16)
            wait(pe, s_wo[b], 32 * (grp // 2 + 1))
            for h in range(HG):
                ins = pe.matmul(PS[h * L:(h + 1) * L, grp, :], WV[:, b, h, :], WO[:, b, h, :], start=True, stop=True)
            s_mm.inc(ins)
            wait(act, s_mm, grp + 1)
            s_mh.inc(act.activation(MH[:, grp, :], PS[:, grp, :], ACT.Copy))
            wait(dve, s_mh, grp + 1)
            s_ml.inc(dve.tensor_tensor(ML[:, grp, :], PS[:, grp, :], MH[:, grp, :].bitcast(F32), ALU.subtract))
        s_ah, s_al, s_y, s_yr, s_yg = (sem(n) for n in ("s_ah", "s_al", "s_y", "s_yr", "s_yg"))
        wait(pe, s_ml, G)
        wait(pool, s_xr, 16)
        pe.sem_inc(s_y.h, 2)
        pool.sem_inc(s_yg.h, 2)

        def tile(st, b):
            src = attn[:, :, bass.ds(st * P, P)]
            wait(act, s_y, st + 1)
            s_ah.inc(act.activation(AH[:, b], src, ACT.Copy))
            wait(dve, s_ah, st + 1)
            s_al.inc(dve.tensor_tensor(AL[:, b], src, AH[:, b].bitcast(F32), ALU.subtract))
            wait(pe, s_al, st + 1)
            for n, (a, w) in enumerate(((AH, MH), (AL, MH), (AH, ML))):
                for grp in range(G):
                    ins = pe.matmul(PS[:, b, :], a[:, b, grp, :], w[:, grp, :],
                                    start=(n == 0 and grp == 0), stop=(n == 2 and grp == G - 1))
            s_y.inc(ins)
            wait(dve, s_y, 2 + st + 1)
            wait(dve, s_yg, st + 1)
            s_yr.inc(dve.tensor_tensor(Y[:, b], PS[:, b, :], gate_a[:], ALU.mult))
            wait(pool, s_yr, st + 1)
            dst = x1[:, bass.ds(st, 1), :].rearrange("p n d -> p (n d)")
            s_yg.inc(pool.tensor_tensor(dst, dst, Y[:, b], ALU.add))

        with nc.Fori(0, NS // 2) as i:
            for b in range(2):
                tile(2 * i + b, b)
        for e in (pe, dve, act, sp):
            wait(e, s_yg, 2 + NS)
    nc.all_engine_barrier()
    normalise_transpose(nc, c, sb, sem, wait, "2", x1, lambda e, st: None, lambda e: None, h2H, h2L, dict(sh, which=2))


def phase_ffn(nc, t, c, sb, sem, wait, sh, out):
    pe, act, dve, pool, sp = nc.tensor, nc.scalar, nc.vector, nc.gpsimd, nc.sync
    g = lambda k: sh[k]
    PS, gate_b, x1, h2H, h2L, ffn_s, s_out = map(g, ("PS", "gate_b", "x1", "h2H", "h2L", "ffn_s", "s_out"))
    NCH = NC + 1
    hid = sh["wide"]
    hid_last = sb("hid_last", [P, S], F32, c)
    DH = sb("DH", [P, NCH, D], F32R, c)
    DL = sb("DL", [P, NCH, D], F32R, c)
    with ExitStack() as m:
        WI = sb("WI", [P, 2, 2, KD, P], I32, m)
        WH = sb("FWH", [P, 2, 2, KD, P], F32R, m)
        WL = sb("FWL", [P, 2, 2, KD, P], F32R, m)
        DI = sb("DI", [P, 2, D], I32, m)
        SG = sb("SG", [P, S], F32, m)
        s_w = [sem("s_fw0"), sem("s_fw1")]
        s_h, s_l, s_dl, s_g, s_u, s_sg, s_hid = (sem(n) for n in ("s_fh", "s_fl", "s_fd", "s_fg", "s_fu", "s_sg", "s_hid"))
        for s, n in ((s_l, 2), (s_dl, 2), (s_hid, 2), (s_u, 2)):
            dve.sem_inc(s.h, n)

        def chunk(ch, b, m_=P):
            lo = ch * P
            wait(sp, s_l, ch + 1)
            wait(sp, s_dl, ch + 1)
            turn = (ch - b) // 2 if isinstance(ch, int) else None
            for w, name in ((0, "gate_w"), (1, "up_w")):
                s_w[b].inc(sp.dma_start(WI[:, b, w, :, 0:m_], t[name][:, :, bass.ds(lo, m_)]), 16)
            s_w[b].inc(sp.dma_start(DI[0:m_, b, :], t["down_w"][bass.ds(lo, m_), :]), 16)
            return turn

        def chunk_work(ch, turn, b, m_=P):
            wait(act, s_w[b], 48 * (turn + 1))
            wait(act, s_u, ch + 1)
            s_h.inc(act.activation(WH[:, b, :, :, 0:m_], WI[:, b, :, :, 0:m_], ACT.Copy))
            wait(dve, s_h, 2 * ch + 1)
            s_l.inc(dve.tensor_tensor(WL[:, b, :, :, 0:m_], WI[:, b, :, :, 0:m_], WH[:, b, :, :, 0:m_].bitcast(F32), ALU.subtract))
            dh = DH[0:m_, bass.ds(ch, 1), :].rearrange("p c d -> p (c d)")
            dl = DL[0:m_, bass.ds(ch, 1), :].rearrange("p c d -> p (c d)")
            s_h.inc(act.activation(dh, DI[0:m_, b, :], ACT.Copy))
            wait(dve, s_h, 2 * ch + 2)
            s_dl.inc(dve.tensor_tensor(dl, DI[0:m_, b, :], dh.bitcast(F32), ALU.subtract))
            wait(pe, s_l, 2 + ch + 1)
            wait(pe, s_hid, ch + 1)
            for w, s in ((0, s_g), (1, s_u)):
                for hf in range(2):
                    for n, (a, h) in enumerate(((WH, h2H), (WL, h2H), (WH, h2L))):
                        for k in range(KD):
                            ins = pe.matmul(PS[0:m_, 4 * b + 2 * w + hf, :], a[:, b, w, k, 0:m_],
                                            h[:, k, hf * 512:(hf + 1) * 512],
                                            start=(n == 0 and k == 0), stop=(n == 2 and k == KD - 1))
                s.inc(ins)
            wait(act, s_g, ch + 1)
            wait(act, s_hid, 2 + ch)
            s_sg.inc(act.activation(SG[0:m_, :].rearrange("p (b n) -> p b n", b=2), PS[0:m_, 4 * b:4 * b + 2, :], ACT.Silu,
                                    scale=ffn_s[0:m_, 0:1]))
            wait(dve, s_sg, ch + 1)
            wait(dve, s_u, 2 + ch + 1)
            s_hid.inc(dve.scalar_tensor_tensor(
                out=hid[:, bass.ds(ch, 1), :].rearrange("p c s -> p (c s)") if m_ == P else hid_last[0:m_, :],
                in0=PS[0:m_, 4 * b + 2:4 * b + 4, :].rearrange("p b n -> p (b n)"), scalar=ffn_s[0:m_, 1:2],
                in1=SG[0:m_, :], op0=ALU.mult, op1=ALU.mult))

        with nc.Fori(0, NC // 2) as i:
            for b in range(2):
                chunk(2 * i + b, b)
            for b in range(2):
                chunk_work(2 * i + b, i, b)
        chunk(NC, 0, IT)
        chunk_work(NC, NC // 2, 0, IT)
        wait(act, s_hid, 2 + NCH)
        wait(dve, s_hid, 2 + NCH)
        wait(pe, s_hid, 2 + NCH)
        wait(sp, s_hid, 2 + NCH)
    nc.all_engine_barrier()
    HH = sb("HH", [P, 2, NCH, P], F32R, c)
    HL = sb("HL", [P, 2, NCH, P], F32R, c)
    Y = sb("Y2", [P, 2, D], F32, c)
    OT = sb("OT", [P, 2, D], F32, c)
    s_hh, s_hl, s_y, s_yr, s_ot = (sem(n) for n in ("s_hh", "s_hl", "s_y2", "s_yr2", "s_ot"))
    pe.sem_inc(s_y.h, 2)
    s_st = [sem("s_store0"), sem("s_store1")]
    dve.sem_inc(s_yr.h, 2)
    pool.sem_inc(s_ot.h, 2)
    for s in s_st:
        sp.sem_inc(s.h, 16)

    def tile(st, i, b):
        wait(act, s_y, st + 1)
        for m_, ch in ((P, slice(0, NC)), (IT, slice(NC, NC + 1))):
            src = hid[:, :, bass.ds(st * P, P)] if m_ == P else hid_last[0:m_, bass.ds(st * P, P)]
            dst = HH[0:m_, b, ch, :] if m_ == P else HH[0:m_, b, NC, :]
            dst_lo = HL[0:m_, b, ch, :] if m_ == P else HL[0:m_, b, NC, :]
            s_hh.inc(act.activation(dst, src, ACT.Copy))
            wait(dve, s_hh, 2 * st + (1 if m_ == P else 2))
            s_hl.inc(dve.tensor_tensor(dst_lo, src, dst.bitcast(F32), ALU.subtract))
        wait(pe, s_hl, 2 * st + 2)
        wait(pe, s_yr, st + 1)
        for n, (a, w) in enumerate(((HH, DH), (HL, DH), (HH, DL))):
            for ch in range(NCH):
                k = P if ch < NC else IT
                ins = pe.matmul(PS[:, b, :], a[0:k, b, ch, :], w[0:k, ch, :],
                                start=(n == 0 and ch == 0), stop=(n == 2 and ch == NCH - 1))
        s_y.inc(ins)
        wait(dve, s_y, 2 + st + 1)
        wait(dve, s_ot, st + 1)
        s_yr.inc(dve.scalar_tensor_tensor(out=Y[:, b], in0=PS[:, b, :], scalar=ffn_s[:, 2:3], in1=gate_b[:],
                                          op0=ALU.mult, op1=ALU.mult))
        wait(pool, s_yr, 2 + st + 1)
        wait(pool, s_st[b], 16 * (i + 1))
        s_ot.inc(pool.tensor_tensor(OT[:, b], x1[:, bass.ds(st, 1), :].rearrange("p n d -> p (n d)"), Y[:, b], ALU.add))
        wait(sp, s_ot, 2 + st + 1)
        s_st[b].inc(sp.dma_start(out[bass.ds(st * P, P), :], OT[:, b]), 16)

    with nc.Fori(0, NS // 2) as i:
        for b in range(2):
            tile(2 * i + b, i, b)
    for b in range(2):
        wait(sp, s_st[b], 16 * (NS // 2 + 1))
    nc.all_engine_barrier()


def rotary_tables():
    dim, base, factor, orig = 2 * HALF, 10000.0, 128.0, 1024

    def corr(r):
        return dim * math.log(orig / (r * 2 * math.pi)) / (2 * math.log(base))
    low, high = max(math.floor(corr(32.0)), 0), min(math.ceil(corr(1.0)), dim - 1)
    hi = high + 0.001 if low == high else float(high)
    ramp = np.clip((np.arange(dim // 2, dtype=np.float32) - low) / (hi - low), 0.0, 1.0)
    keep = 1.0 - ramp
    extra = 1.0 / base ** (np.arange(0, dim, 2, dtype=np.float32) / dim)
    inv = extra / factor * (1.0 - keep) + extra * keep
    freqs = np.outer(np.arange(S, dtype=np.float32), inv)
    return np.cos(freqs).astype(np.float32), np.sin(freqs).astype(np.float32)


def kernel(**inputs):
    import concourse.bacc as bacc
    from concourse.bass_utils import run_bass_kernel_spmd

    a = {k: np.asarray(v) for k, v in inputs.items()}
    cosT, sinT = (m.T for m in rotary_tables())
    wq = a["L0_attn_wq_b"].reshape(G, HG, NOPE + 2 * HALF, R)
    pe_rows = wq[:, :, NOPE:, :].reshape(G, HG, HALF, 2, R)
    wkv = a["L0_attn_wkv_b"].reshape(G, HG, NOPE + VD, L)
    ckv, kpe = a["L0_attn_wkv_a"][:L], a["L0_attn_wkv_a"][L:]
    wa = np.concatenate([a["L0_attn_wq_a"], kpe[0::2], kpe[1::2], ckv, kpe[1::2], kpe[0::2]], 0)
    chunks = lambda w: w.T.reshape(KD, P, -1).transpose(1, 0, 2)
    t = {
        "x": a["L0_attn_x"][0],
        "c": a["L0_c"].reshape(KD, P).T,
        "wmod": a["L0_wmod"].reshape(KD, P, 6, D).transpose(2, 1, 0, 3),
        "wa": chunks(wa),
        "lnq": a["L0_attn_q_a_ln_w"].reshape(R, 1),
        "lnkv": a["L0_attn_kv_a_ln_w"].reshape(L, 1),
        "ffn_s": np.tile(np.concatenate([a["L0_ffn_gate_s"], a["L0_ffn_up_s"], a["L0_ffn_down_s"]]), (P, 1)),
        "cos": np.tile(cosT, (4, 1)),
        "sin": np.tile(sinT, (4, 1)),
        "swap_sin": np.concatenate([-sinT, sinT], 0),
        "wq_pe": pe_rows.transpose(0, 4, 3, 1, 2).reshape(G, R, 2 * P),
        "wq_nope": wq[:, :, :NOPE, :].transpose(0, 2, 1, 3).reshape(G, NOPE, HG * R),
        "wk": wkv[:, :, :NOPE, :].transpose(0, 2, 1, 3).reshape(G, NOPE, HG * L),
        "wv": wkv[:, :, NOPE:, :].transpose(0, 2, 1, 3).reshape(G, VD, HG * L),
        "wo": a["L0_attn_wo"].reshape(D, G, HG, VD).transpose(1, 3, 2, 0).reshape(G, VD, HG * D),
        "gate_w": chunks(a["L0_ffn_gate_w"]),
        "up_w": chunks(a["L0_ffn_up_w"]),
        "down_w": a["L0_ffn_down_w"].T,
    }
    nc = bacc.Bacc("TRN2", target_bir_lowering=False, num_devices=1)
    arrays, aps = {}, {}
    for name, v in t.items():
        v = np.ascontiguousarray(v)
        arrays["in_" + name] = v
        aps[name] = nc.dram_tensor("in_" + name, v.shape, mybir.dt.from_np(v.dtype), kind="ExternalInput").ap()
    out = nc.dram_tensor("out_0", (S, D), F32, kind="ExternalOutput").ap()
    build(nc, aps, out)
    r = run_bass_kernel_spmd(nc, [arrays], core_ids=[0])
    return r.results[0]["out_0"].reshape(1, S, D)
```

```python
import concourse.bass as bass
from concourse import mybir
from concourse.alu_op_type import AluOpType as ALU
from contextlib import ExitStack
import math
import numpy as np

F32 = mybir.dt.float32
F32R = mybir.dt.float32r
BF16 = mybir.dt.bfloat16
I32 = mybir.dt.int32
ACT = mybir.ActivationFunctionType
AX = mybir.AxisListType

P = 128
S, D, H = 1024, 512, 32
R, L, HALF = 128, 32, 32
NOPE, VD = 64, 128
I = 1376
G, HG = 8, 4
KR = 2 * HALF + L
KD = D // P
NS = S // P
QB = 512
NQB = S // QB
NC, IT = I // P, I % P
EPS_RMS, EPS_LN = 1e-6, 1e-5
FLOOR = 0.25
MASKED = -1e30
STEPS = [(qb, kt) for qb in range(NQB) for kt in range((qb + 1) * QB // P)]
NSTEP = len(STEPS)
WINDOW_US = 56.0
POOL_HEADS = 2
SLACK = 0.04


def softmax_scale():
    m = 0.1 * math.log(128.0) + 1.0
    return (NOPE + 2 * HALF) ** -0.5 * m * m


def width(qb, kt):
    return min(QB, (qb + 1) * QB - kt * P)


class Count:

    def __init__(self, handle):
        self.h, self.n = handle, 0

    def inc(self, ins, k=1):
        ins.then_inc(self.h, k)
        self.n += k
        return self.n


def build(nc, t, out):
    pe, act, dve, pool, sp = nc.tensor, nc.scalar, nc.vector, nc.gpsimd, nc.sync
    top = ExitStack()
    with top:
        def sem(name):
            return Count(top.enter_context(nc.semaphore(name)))

        def sb(name, shape, dt=F32, where=top, side=None):
            if side:
                return where.enter_context(nc.sbuf_tensor(name, shape, dt, side=side))
            return where.enter_context(nc.sbuf_tensor(name, shape, dt))

        s_seen = [sem("s_seen_pool"), sem("s_seen_sp"), sem("s_seen_dve")]

        def wait(eng, s, value, alone=False):
            eng.wait_ge(s.h, value)
            if not isinstance(value, int) and (alone or eng in (sp, pool)):
                eng.sem_inc(s_seen[(pool, sp, dve).index(eng)].h, 1)

        PS = top.enter_context(nc.psum_tensor("PS", [P, 8, 512], F32))
        ident = sb("ident", [P, P])
        ones = sb("ones", [P, P])
        gate_a = sb("gate_a", [P, D])
        gate_b = sb("gate_b", [P, D])
        lnq = sb("lnq", [P, 1])
        cT = sb("cT", [P, KD])
        silu_c = sb("silu_c", [P, KD])
        ffn_s = sb("ffn_s", [P, 3])
        mod_col = sb("mod_col", [P, 4, KD])
        eps = sb("eps", [P, 2])
        stats = sb("stats", [P, NS, 6])
        mv = sb("mv", [P, NS, 2])
        rstd = sb("rstd", [P, NS])
        Q = sb("Q", [P, 2, 2, HG, S], F32R, top, "right")
        TQ = sb("TQ", [P, 3, 2, S], F32R, top, "right")
        x1 = TQ[:, 0:2].bitcast(F32).rearrange("p b l (n d) -> p (b l n) d", d=D)
        wo_slot = TQ[:, 2].bitcast(F32)
        MH = Q[:, 0, 0].rearrange("p h (n d) -> p (h n) d", d=D)
        ML = Q[:, 0, 1].rearrange("p h (n d) -> p (h n) d", d=D)
        h2H, h2L = Q[:, 1, 0], Q[:, 1, 1]

        s_const, s_small = sem("s_const"), sem("s_small")
        s_k1 = sem("s_k1")
        s_tables = sem("s_tables")
        s_scb = sem("s_scb")
        s_ql = sem("s_ql")
        s_xr = sem("s_xr")
        s_tiles = sem("s_tiles")

        s_const.inc(pool.memset(ident[:], 0.0))
        s_const.inc(pool.memset(ones[:], 1.0))
        s_const.inc(pool.memset(eps[:, 0:1], EPS_RMS))
        s_const.inc(pool.memset(eps[:, 1:2], EPS_LN))
        wait(pool, s_const, 4)
        s_const.inc(pool.affine_select(out=ident[:], in_=ident[:], compare_op=ALU.not_equal, fill=1.0,
                                       base=0, pattern=[[-1, P]], channel_multiplier=1))

        with ExitStack() as shared:
            KH = sb("KH", [P, S], F32R, shared)
            KL = sb("KL", [P, S], F32R, shared)
            V = sb("V", [P, NS, L], F32, shared)
            QNH = sb("QNH", [P, S], F32R, shared)
            QNL = sb("QNL", [P, S], F32R, shared)
            cos = sb("cos", [P, S], F32, shared)
            sin = sb("sin", [P, S], F32, shared)

            PR = sb("PR", [P, 3, HG, QB], F32, shared)
            RD = sb("RD", [P, QB], F32, shared)
            scb = RD[:].rearrange("p (k n) -> p k n", k=KD)
            load_mod, mod_columns, mod_rows, s_wm, s_m, s_mc = modulations(nc, t, sem, wait, locals())
            with ExitStack() as c:
                phase_inputs(nc, t, c, sb, sem, wait, locals())
            wide = sb("wide", [P, NC, S], F32, top, "right")
            attn = wide[:, 0:G, :]
            with ExitStack() as c:
                done = phase_attention(nc, t, c, sb, sem, wait, locals())
        WI = sb("WI", [P, 2, 2, KD, P], I32)
        DI = sb("DI", [P, 2, D], I32)
        with ExitStack() as c:
            last = phase_project(nc, t, c, sb, sem, wait, locals())
        phase_ffn(nc, t, sb, sem, wait, locals(), out)


def phase_inputs(nc, t, c, sb, sem, wait, sh):
    pe, act, dve, pool, sp = nc.tensor, nc.scalar, nc.vector, nc.gpsimd, nc.sync
    g = lambda k: sh[k]
    PS, ident, ones, KH, KL, V, QNH, QNL, cos, sin = map(g, ("PS", "ident", "ones", "KH", "KL", "V", "QNH", "QNL", "cos", "sin"))
    lnq, ffn_s, mod_col, eps, Q, PR, x, scb = map(g, ("lnq", "ffn_s", "mod_col", "eps", "Q", "PR", "x1", "scb"))
    stats, mv, rstd, s_const, s_small = map(g, ("stats", "mv", "rstd", "s_const", "s_small"))
    ROWS = R + KR + 2 * HALF
    KV = R + 2 * HALF
    cT, silu_c = g("cT"), g("silu_c")
    WA = sb("WA", [P, KD, ROWS], F32, c, "right")
    WAH = sb("WAH", [P, KD, ROWS], F32R, c, "right")
    WAL = sb("WAL", [P, KD, ROWS], F32R, c, "right")
    xn = sb("xn1", [P, 2, D], F32, c, "right")
    full = sb("full1", [P, 2, KD, P], F32, c, "right")
    hH = sb("hH", [P, 2, KD, P], F32R, c, "right")
    hL = sb("hL", [P, 2, KD, P], F32R, c, "right")
    rope_k = sb("rope_k", [P, NS, 2, 2 * HALF], F32, c, "right")
    lnkv = sb("lnkv", [P, L], F32, c, "right")
    squares = sb("squares", [P, 2, R + L], F32, c, "right")
    ms = sb("ms", [P, 2, 2], F32, c, "right")
    rms = sb("rms", [P, 2, 2], F32, c, "right")
    qn = sb("qn", [P, 2, R], F32, c, "right")
    rot = sb("rot", [P, 2, 2, 2 * HALF], F32, c, "right")
    key = sb("key", [P, 2, KR], F32, c, "right")

    s_xh = [sem("s_xh0"), sem("s_xh1")]
    s_wm = g("s_wm")
    s_wa, s_rope = sem("s_wa"), sem("s_rope")
    s_c = sem("s_c")
    s_c.inc(sp.dma_start(cT[:], t["c"]), 16)
    xt = t["x"].rearrange("(n p) d -> p n d", p=P)
    for hf in range(2):
        half = slice(hf * NS // 2, (hf + 1) * NS // 2)
        s_xh[hf].inc(act.dma_start(x[:, half, :], xt[:, half, :]), 16)
    load_mod = g("load_mod")
    load_mod(0)
    load_mod(1)
    s_wa.inc(act.dma_start(WA[:], t["wa"]), 16)
    for dst, name in ((lnq, "lnq"), (lnkv, "lnkv"), (ffn_s, "ffn_s")):
        s_small.inc(sp.dma_start(dst[:], t[name]), 16)
    s_rope.inc(sp.dma_start(rope_k[:], t["rope_k"]), 16)
    for n in (2, 3, 4):
        load_mod(n)
    s_tables = g("s_tables")
    s_tables.inc(sp.dma_start(cos[:], t["cos"]), 16)
    s_tables.inc(sp.dma_start(sin[:], t["sin"]), 16)

    s_k1 = g("s_k1")
    wait(pool, s_const, 5)
    for rows, value in [(KH[KR:, :], 0.0), (KL[KR:, :], 0.0), (KH[KR:KR + 1, :], 1.0)] + [
            (Q[KR:, par, hl], 0.0) for par in range(2) for hl in range(2)]:
        s_k1.inc(pool.memset(rows.bitcast(F32), value))
        wait(pool, s_k1, s_k1.n)

    wait(act, s_const, 5)
    wait(act, s_c, 16)
    s_c.inc(act.activation(silu_c[:], cT[:], ACT.Silu))

    s_mv, s_sq, s_rs, s_xn = (sem(n) for n in ("s_mv1", "s_sq1", "s_rs1", "s_xn1"))
    tile_of = lambda st: x[:, bass.ds(st, 1), :].rearrange("p n d -> p (n d)")
    one = lambda ap, st: ap[:, bass.ds(st, 1)]
    N2 = NS // 2
    for hf in range(2):
        half = slice(hf * N2, (hf + 1) * N2)
        wait(dve, s_xh[hf], 16)
        for st in range(hf * N2, (hf + 1) * N2):
            s_mv.inc(dve.bn_stats(stats[:, st, :], x[:, st, :]))
            wait(dve, s_mv, s_mv.n)
            s_mv.inc(dve.bn_aggr(mv[:, st, :], stats[:, st, :]))
        wait(act, s_mv, NS * (hf + 1))
        s_sq.inc(act.activation(rstd[:, half], mv[:, half, 1], ACT.Sqrt, bias=eps[:, 1:2]))
        wait(dve, s_sq, hf + 1)
        s_rs.inc(dve.reciprocal(rstd[:, half], rstd[:, half]))
    wait(dve, s_small, 48)
    wait(dve, s_const, 5)
    wait(dve, s_c, 17)
    for k in range(KD):
        last = dve.tensor_scalar(scb[:, k, :], ones[:], silu_c[:, k:k + 1], None, ALU.mult)
    g("s_scb").inc(last)
    dve.tensor_scalar(lnq[:], lnq[:], softmax_scale(), None, ALU.mult)

    wait(pe, s_const, 5)
    wait(pe, s_c, 17)
    for n in range(2):
        for d in range(KD):
            g("mod_columns")(n, d, PS[:, 6 + n, 0:KD])

    s_wah, s_wal = sem("s_wah"), sem("s_wal")
    wait(act, s_wa, 16)
    s_wah.inc(act.activation(WAH[:], WA[:], ACT.Copy))
    wait(pool, s_wah, 1)
    s_wal.inc(pool.tensor_tensor(WAL[:], WA[:], WAH[:].bitcast(F32), ALU.subtract))

    s_tr = sem("s_tr1")
    s_full = sem("s_full1")
    s_hi = sem("s_hi1")
    s_lo = sem("s_lo1")
    s_pj = sem("s_pj")
    s_ss = sem("s_ss")
    s_rt = sem("s_rt")
    s_inv = sem("s_inv")
    s_cr = sem("s_cr")
    s_kr = sem("s_kr")
    s_t2 = sem("s_t2")
    s_qh = sem("s_qh")
    s_ql = g("s_ql")
    for e, s in ((pe, s_tr), (act, s_full), (pool, s_lo), (pe, s_pj), (dve, s_cr), (pe, s_t2), (dve, s_ql)):
        e.sem_inc(s.h, 2)
    wait(act, g("s_mc"), 2)
    wait(dve, s_rope, 16)
    wait(dve, s_rs, 2)

    def normalise(st, b):
        wait(dve, s_tr, st + 1)
        s_xn.inc(dve.tensor_scalar(xn[:, b, :], tile_of(st), one(mv, st)[:, 0, 0:1], one(rstd, st),
                                   ALU.subtract, ALU.mult))

    def modulate(st, b):
        wait(pe, s_xn, st + 1)
        wait(pe, s_full, st + 1)
        for d in range(KD):
            ins = pe.transpose(PS[:, b, d * P:(d + 1) * P], xn[:, b, d * P:(d + 1) * P], ident[:])
        s_tr.inc(ins)
        wait(act, s_tr, 2 + st + 1)
        wait(act, s_lo, st + 1)
        for d in range(KD):
            ins = act.activation(full[:, b, d, :], PS[:, b, d * P:(d + 1) * P], ACT.Identity,
                                 scale=mod_col[:, 0, d:d + 1], bias=mod_col[:, 1, d:d + 1])
        s_full.inc(ins)
    def split(st, b):
        wait(dve, s_full, 2 + st + 1)
        wait(dve, s_pj, st + 1)
        s_hi.inc(dve.tensor_copy(hH[:, b], full[:, b]))
        wait(pool, s_hi, st + 1)
        s_lo.inc(pool.tensor_tensor(hL[:, b], full[:, b], hH[:, b].bitcast(F32), ALU.subtract))

    def project(st, b):
        wait(pe, s_lo, 2 + st + 1)
        if isinstance(st, int) and st == 0:
            wait(pe, s_wal, 1)
        wait(pe, s_cr, st + 1)
        bank = PS[:, 2 + b, :]
        for n, (h, w) in enumerate(((hH, WAH), (hL, WAH), (hH, WAL))):
            for k in range(KD):
                ins = pe.matmul(bank[:, 0:ROWS], h[:, b, k, :], w[:, k, :], start=(n == 0 and k == 0),
                                stop=(n == 2 and k == KD - 1))
        s_pj.inc(ins)

    def scale(st, b):
        bank = PS[:, 2 + b, :]
        wait(act, s_pj, 2 + st + 1)
        wait(act, s_inv, st + 1)
        s_ss.inc(act.activation(squares[:, b, 0:R], bank[:, 0:R], ACT.Square, accum_out=ms[:, b, 0:1]))
        s_ss.inc(act.activation(squares[:, b, R:], bank[:, KV:KV + L], ACT.Square, accum_out=ms[:, b, 1:2]))
        wait(act, s_ss, 2 * st + 2)
        s_rt.inc(act.activation(rms[:, b, 0:1], ms[:, b, 0:1], ACT.Sqrt, scale=1.0 / R, bias=eps[:, 0:1]))
        s_rt.inc(act.activation(rms[:, b, 1:2], ms[:, b, 1:2], ACT.Sqrt, scale=1.0 / L, bias=eps[:, 0:1]))
        wait(dve, s_rt, 2 * st + 2)
        s_inv.inc(dve.reciprocal(rms[:, b, :], rms[:, b, :]))
        wait(dve, s_t2, st + 1)
        dve.tensor_tensor(rot[:, b, 0, :], bank[:, R:KV], one(rope_k, st)[:, 0, 0, :], ALU.mult)
        dve.tensor_tensor(rot[:, b, 1, :], bank[:, KV + L:ROWS], one(rope_k, st)[:, 0, 1, :], ALU.mult)
        wait(dve, s_inv, 2 + st + 1)
        dve.tensor_scalar(qn[:, b, :], bank[:, 0:R], rms[:, b, 0:1], None, ALU.mult)
        s_cr.inc(dve.scalar_tensor_tensor(out=key[:, b, 2 * HALF:], in0=bank[:, KV:KV + L], scalar=rms[:, b, 1:2],
                                          in1=lnkv[:], op0=ALU.mult, op1=ALU.mult))
        wait(dve, s_cr, 2 + st + 1)
        dve.tensor_copy(one(V, st)[:, 0, :], key[:, b, 2 * HALF:])
        s_kr.inc(dve.tensor_tensor(key[:, b, 0:2 * HALF], rot[:, b, 0, :], rot[:, b, 1, :], ALU.add))

    def turn(st, b):
        wait(pe, s_kr, st + 1)
        wait(pe, s_ql, st + 1)
        bank = PS[:, 4 + b, :]
        pe.transpose(bank[:, 0:P], qn[:, b, :], ident[:])
        s_t2.inc(pe.transpose(bank[0:KR, P:2 * P], key[:, b, :], ident[:]))
    def split_latents(st, b):
        cols = bass.ds(st * P, P)
        bank = PS[:, 4 + b, :]
        wait(act, s_t2, 2 + st + 1)
        act.activation(QNH[:, cols], bank[:, 0:P], ACT.Copy)
        s_qh.inc(act.activation(KH[0:KR, cols], bank[0:KR, P:2 * P], ACT.Copy))
        wait(dve, s_qh, st + 1)
        dve.tensor_tensor(QNL[:, cols], bank[:, 0:P], QNH[:, cols].bitcast(F32), ALU.subtract)
        s_ql.inc(dve.tensor_tensor(KL[0:KR, cols], bank[0:KR, P:2 * P], KH[0:KR, cols].bitcast(F32), ALU.subtract))

    def step(st, b, within=lambda n: 0 <= n < NS):
        for stage, back in ((normalise, -1), (modulate, 0), (project, 1), (turn, 3), (scale, 2), (split, 0),
                            (split_latents, 3)):
            if not isinstance(st, int) or within(st - back):
                stage(st - back, b if back % 2 == 0 else 1 - b)

    dve.sem_inc(s_inv.h, 2)
    first = 4
    normalise(0, 0)
    for st in range(first):
        step(st, st % 2)
    with nc.Fori(0, (NS - 1 - first) // 2) as i:
        step(2 * i + first, 0)
        step(2 * i + first + 1, 1)
    for st in range(NS - 2, NS + 3):
        step(st, st % 2)


def modulations(nc, t, sem, wait, sh):
    pe, act, dve, sp = nc.tensor, nc.scalar, nc.vector, nc.sync
    PR, mod_col, silu_c, scb = (sh[k] for k in ("PR", "mod_col", "silu_c", "scb"))
    ORDER = [1, 0, 4, 3, 2, 5]
    s_wm = [sem(f"s_wm{i}") for i in range(6)]
    s_m = sem("s_m")
    s_mc = sem("s_mc")

    def load_mod(n):
        if n >= 3:
            wait(sp, s_m, n - 2)
        s_wm[n].inc(sp.dma_start(PR[:, n % 3], t["wmod"][ORDER[n]]), 16)

    def mod_columns(n, d, dst):
        wait(pe, s_wm[n], 16)
        wait(pe, s_mc, max(n - 1, 0))
        for k in range(KD):
            ins = pe.matmul(dst[:, d:d + 1], PR[:, n % 3, k, d * P:(d + 1) * P], silu_c[:, k:k + 1],
                            start=(k == 0), stop=(k == KD - 1))
        if d < KD - 1:
            return
        s_m.inc(ins)
        wait(dve, s_m, n + 1)
        s_mc.inc(dve.tensor_scalar(mod_col[:, n, :], dst, 1.0 if n % 2 == 0 else 0.0, None, ALU.add))

    def mod_rows(n, k, bank, dst):
        wait(pe, s_wm[n], 16)
        wait(pe, s_mc, max(n - 1, 0))
        ins = pe.matmul(bank, scb[:, k, :], PR[:, n % 3, k, :], start=(k == 0), stop=(k == KD - 1))
        if k < KD - 1:
            return
        s_m.inc(ins)
        wait(dve, s_m, n + 1)
        s_mc.inc(dve.tensor_copy(dst[:], bank))
    return load_mod, mod_columns, mod_rows, s_wm, s_m, s_mc


def phase_attention(nc, t, c, sb, sem, wait, sh):
    pe, act, dve, pool, sp = nc.tensor, nc.scalar, nc.vector, nc.gpsimd, nc.sync
    g = lambda k: sh[k]
    PS, ident, ones, KH, KL, V, QNH, QNL, cos, sin = map(g, ("PS", "ident", "ones", "KH", "KL", "V", "QNH", "QNL", "cos", "sin"))
    lnq, attn, Q, TQ, PR, RD = map(g, ("lnq", "attn", "Q", "TQ", "PR", "RD"))
    WP = sb("WP", [P, 2 * P], F32, c)
    WN = sb("WN", [NOPE, HG, R], F32, c)
    WK = sb("WK", [NOPE, HG, L], F32, c)
    WF = sb("WF", [P, 3 * P], F32, c)
    WH = sb("WH", [P, 3 * P], F32R, c)
    WL = sb("WL", [P, 3 * P], F32R, c)
    RT = sb("RT", [P, 4, 512], F32, c)
    RE = sb("RE", [P, 2, 512], F32, c)
    NMa = sb("NMa", [P, HG, NS], F32, c)
    NMb = sb("NMb", [P, HG, NS // 2], F32, c)
    NM = sb("NM", [HG * NS, P], F32R, c)
    identb = sb("identb", [P, P], BF16, c)
    maskb = sb("maskb", [P, P], BF16, c)

    s_w = sem("s_w")
    s_wf = sem("s_wf")
    s_wh = sem("s_wh")
    s_wl = sem("s_wl")
    s_af = sem("s_af")
    s_ar = sem("s_ar")
    s_re = sem("s_re")
    s_th = sem("s_th")
    s_lh = sem("s_lh")
    s_tl = sem("s_tl")
    s_q = [sem(f"s_q{h}") for h in range(HG)]
    s_nm = sem("s_nm")
    s_nd = sem("s_nd")
    s_st = sem("s_st")
    s_p = sem("s_p")
    s_pv = sem("s_pv")
    s_ad = sem("s_ad")
    s_ae = sem("s_ae")
    s_o = sem("s_o")
    s_rd = sem("s_rd")
    s_no = sem("s_no")
    s_mk = sem("s_mk")
    s_wo = [sem("s_wo0"), sem("s_wo1")]
    s_wv = sem("s_wv")
    s_mh = sem("s_mh")
    s_gt = sem("s_gt")
    WO = [RT[:], g("wo_slot").rearrange("p l (n d) -> p (l n) d", d=D)]
    WV = RE[:].rearrange("p a (g h l) -> p (a g) h l", h=HG, l=L)
    UQ = 3 + 3 * NQB
    UM = HG * (NS + NS // 2) + 1
    UW = UQ + UM + NQB
    U0 = 2 * UQ + UM
    assert UW % 3 == 0
    SUM = [g("wide")[:, G:G + 2, :].rearrange("p c (h q) -> p (c h) q", q=QB), PR[:, 2]]
    ADDS = [s for s in range(NSTEP) if STEPS[s][1] > 0]
    NADD = len(ADDS)
    NPAIR = 2 * NSTEP

    s_mk.inc(pool.memset(identb[:], 0.0))
    s_mk.inc(pool.memset(maskb[:], 0.0))
    wait(pool, s_mk, 2)
    s_mk.inc(pool.affine_select(out=identb[:], in_=identb[:], compare_op=ALU.not_equal, fill=1.0, base=0,
                                pattern=[[-1, P]], channel_multiplier=1))
    s_mk.inc(pool.affine_select(out=maskb[:], in_=maskb[:], compare_op=ALU.is_ge, fill=MASKED, base=0,
                                pattern=[[-1, P]], channel_multiplier=1))
    wait(pe, s_mk, 4)
    wait(pe, g("s_k1"), 7)
    wait(sp, g("s_k1"), 7)
    wait(pe, g("s_ql"), 2 + NS)
    wait(pe, g("s_scb"), 1)
    wait(dve, g("s_tables"), 32)
    dve.sem_inc(s_ar.h, 3)
    dve.sem_inc(s_rd.h, 8)
    dve.sem_inc(s_ae.h, 2)
    pool.sem_inc(s_ad.h, 2)
    act.sem_inc(s_o.h, 1)
    pool.sem_inc(s_no.h, 1)
    pool.sem_inc(s_wl.h, 1)
    pool.sem_inc(s_re.h, 1)
    pool.sem_inc(s_tl.h, 1)
    sp.sem_inc(s_nd.h, 16)
    for h in range(HG):
        sp.sem_inc(s_q[h].h, 48)
    act.sem_inc(s_p.h, 2)
    pe.sem_inc(s_pv.h, 3)
    pe.sem_inc(s_st.h, NPAIR)

    def load_weights(grp):
        s_w.inc(sp.dma_start(WP[:], t["wq_pe"][bass.ds(grp, 1)].rearrange("g p n -> (g p) n")), 16)
        s_w.inc(sp.dma_start(WN[:].rearrange("p h r -> p (h r)"),
                             t["wq_nope"][bass.ds(grp, 1)].rearrange("g p n -> (g p) n")), 16)
        s_w.inc(sp.dma_start(WK[:].rearrange("p h r -> p (h r)"),
                             t["wk"][bass.ds(grp, 1)].rearrange("g p n -> (g p) n")), 16)

    def send_queries(grp, par):
        wait(sp, s_tl, 1 + 2 * (grp + 1))
        if not isinstance(grp, int) or grp > 1:
            wait(sp, s_st, NPAIR + NPAIR * (grp - 1))
        for h in range(HG):
            for b in range(3):
                s_q[h].inc(sp.dma_start(Q[b * 32:(b + 1) * 32, par, :, h, :].bitcast(F32),
                                        TQ[h * 32:(h + 1) * 32, b, :, :].bitcast(F32)), 16)

    class Side:

        def __init__(self, first, turn):
            self.first, self.turn, self.at = first, turn % 3, 0

        def take(self):
            n, u = self.first + self.at, (self.turn + self.at) % 3
            self.at += 1
            wait(pe, s_ar, n + 1)
            return n, PS[:, 5 + u, :]

    def queries(side, grp, first=False):

        def weights(h0, h1):
            n, bank = side.take()
            wait(pe, s_w, 48 * (grp + 1))
            for h in range(h0, h1):
                ins = pe.matmul(bank[:, h * L:(h + 1) * L], WN[:, h, :], WK[:, h, :], start=True, stop=True)
            s_af.inc(ins)
            if h0 == 0:
                wait(dve, s_w, 48 * (grp + 1))
                wait(dve, s_wl, 1 + grp)
                s_wf.inc(dve.tensor_scalar(WF[:, 0:2 * P], WP[:], lnq[:], None, ALU.mult))
            wait(dve, s_af, n + 1)
            s_ar.inc(dve.tensor_scalar(WF[:, 2 * P + h0 * L:2 * P + h1 * L], bank[:, h0 * L:h1 * L], lnq[:], None, ALU.mult))
            if h1 < HG:
                return
            wait(act, s_wf, grp + 1)
            wait(act, s_ar, 3 + n + 1)
            s_wh.inc(act.activation(WH[:], WF[:], ACT.Copy))
            wait(pool, s_wh, grp + 1)
            s_wl.inc(pool.tensor_tensor(WL[:], WF[:], WH[:].bitcast(F32), ALU.subtract))

        def project(block, hf):
            cols = slice(hf * 512, hf * 512 + 512)
            n, bank = side.take()
            wait(pe, s_wl, 1 + grp + 1)
            for k, (w, q) in enumerate(((WH, QNH), (WL, QNH), (WH, QNL))):
                ins = pe.matmul(bank, w[:, block * P:(block + 1) * P], q[:, cols], start=(k == 0), stop=(k == 2))
            s_af.inc(ins)
            return n, bank

        def even(hf):
            cols = slice(hf * 512, hf * 512 + 512)
            n, bank = project(0, hf)
            wait(dve, s_af, n + 1)
            wait(dve, s_re, 2 * (2 * grp + hf) + 1)
            dve.tensor_tensor(RT[:, 0, :], bank, cos[:, cols], ALU.mult)
            s_ar.inc(dve.tensor_tensor(RT[:, 3, :], bank, sin[:, cols], ALU.mult))

        def odd(hf):
            cols = slice(hf * 512, hf * 512 + 512)
            half = 2 * grp + hf
            n, bank = project(1, hf)
            wait(dve, s_af, n + 1)
            dve.tensor_tensor(RT[:, 1, :], bank, sin[:, cols], ALU.mult)
            s_ar.inc(dve.tensor_tensor(RT[:, 2, :], bank, cos[:, cols], ALU.mult))
            eng = dve if first else pool
            wait(eng, s_ar, 3 + n + 1)
            wait(eng, s_tl, half + 1)
            s_re.inc(eng.tensor_tensor(RE[:, 0, :], RT[:, 0, :], RT[:, 1, :], ALU.subtract))
            s_re.inc(eng.tensor_tensor(RE[:, 1, :], RT[:, 2, :], RT[:, 3, :], ALU.add))

        def latent(hf):
            cols = slice(hf * 512, hf * 512 + 512)
            n, bank = project(2, hf)
            if hf == 0:
                for h in range(HG):
                    wait(dve, s_q[h], 48 * (grp + 1))
            wait(dve, s_af, n + 1)
            s_lh.inc(dve.tensor_copy(TQ[:, 2, 0, cols], bank))
            wait(dve, s_lh, 2 * grp + hf + 1)
            s_ar.inc(dve.tensor_tensor(TQ[:, 2, 1, cols], bank, TQ[:, 2, 0, cols].bitcast(F32), ALU.subtract))
            wait(pool, s_ar, 3 + n + 1)

        def split(hf):
            cols = slice(hf * 512, hf * 512 + 512)
            half = 2 * grp + hf
            if hf == 0:
                for h in range(HG):
                    wait(act, s_q[h], 48 * (grp + 1))
            wait(act, s_re, 1 + 2 * half + 2)
            s_th.inc(act.activation(TQ[:, 0:2, 0, cols], RE[:], ACT.Copy))
            eng = dve if first else pool
            if first:
                wait(dve, s_ar, 3 + s_ar.n)
            wait(eng, s_th, half + 1)
            s_tl.inc(eng.tensor_tensor(TQ[:, 0:2, 1, cols], RE[:], TQ[:, 0:2, 0, cols].bitcast(F32), ALU.subtract))

        return [(0.13, lambda: weights(0, 2), 0.5), (0.14, lambda: weights(2, 3), 0.15),
                (0.15, lambda: weights(3, 4), 0.15), (0.25, lambda: even(0), 1.2), (0.28, lambda: odd(0), 1.2),
                (0.36, lambda: latent(0), 1.3), (0.40, lambda: split(0), 0.0), (0.54, lambda: even(1), 1.2),
                (0.57, lambda: odd(1), 1.2), (0.65, lambda: latent(1), 1.3), (0.75, lambda: split(1), 0.0)]

    def maxima(side, grp, par):

        def part_of(h, qt, part):
            n, bank = side.take()
            wait(pe, s_q[h], 48 * (grp + 2))
            lo = part * 512
            w = min(512, (qt + 1) * P - lo)
            diagonal = (qt + 1) * P == lo + w
            ins = pe.matmul(bank[:, 0:w], Q[0:KR, par, 0, h, qt * P:(qt + 1) * P], KH[0:KR, lo:lo + w],
                            start=True, stop=not diagonal)
            if diagonal:
                ins = pe.matmul(bank[:, w - P:w], identb[:], maskb[:], start=False, stop=True)
            s_af.inc(ins)
            wait(dve, s_af, n + 1)
            dst = NMb[:, h, qt - NS // 2:qt - NS // 2 + 1] if part else NMa[:, h, qt:qt + 1]
            s_ar.inc(dve.tensor_reduce(dst, bank[:, 0:w], axis=AX.X, op=ALU.max, negate=True))

        def combine():
            wait(dve, s_ar, 3 + side.first + side.at)
            s_nm.inc(dve.tensor_tensor(NMa[:, :, NS // 2:], NMa[:, :, NS // 2:], NMb[:], ALU.min))

        def rows():
            n, bank = side.take()
            wait(pe, s_nm, grp + 1)
            s_af.inc(pe.transpose(bank[0:HG * NS, 0:P], NMa[:].rearrange("p h n -> p (h n)"), ident[:]))
            wait(dve, s_af, n + 1)
            wait(dve, s_nd, 16 * (grp + 1))
            s_ar.inc(dve.tensor_copy(NM[:], bank[0:HG * NS, 0:P]))
            wait(sp, s_ar, 3 + n + 1)
            s_nd.inc(sp.dma_start(Q[KR:KR + 1, par, 0, :, :].rearrange("p h (n q) -> p (h n) q", q=P).bitcast(F32),
                                  NM[:].bitcast(F32)), 16)

        parts = [(h, qt, part) for h in range(HG) for qt in range(NS) for part in range(1 + qt * P // 512)]
        cost = [0.12 + min(512, (qt + 1) * P - part * 512) / 960 for _, qt, part in parts]
        begin, end = 0.1, 0.84
        work = []
        for k, (h, qt, part) in enumerate(parts):
            work.append((begin + (end - begin) * sum(cost[:k]) / sum(cost),
                         lambda h=h, qt=qt, part=part: part_of(h, qt, part), cost[k]))
        return work + [(end + 0.01, combine, 0.1), (end + 0.02, rows, 0.3)]

    def load_wo(m):
        s_wo[m % 2].inc(sp.dma_start(WO[m % 2], t["wo"][m].rearrange("p (h d) -> p h d", h=HG)), 16)

    def load_late():
        for h in range(HG):
            wait(sp, s_q[h], 48 * (G + 1))
        s_xr = g("s_xr")
        s_xr.inc(sp.dma_start(g("x1"), t["x"].rearrange("(n p) d -> p n d", p=P)), 16)
        s_wv.inc(sp.dma_start(RE[:].rearrange("p a b -> p (a b)"), t["wv"]), 16)
        for m in range(2):
            load_wo(m)

    def fold_values(side):
        MH, ML = g("MH"), g("ML")

        def fold(m):
            n, bank = side.take()
            wait(pe, s_wv, 16)
            wait(pe, s_wo[m % 2], 16 * (m // 2 + 1))
            for h in range(HG):
                ins = pe.matmul(bank[h * L:(h + 1) * L, :], WV[:, m, h, :], WO[m % 2][:, h, :], start=True, stop=True)
            s_af.inc(ins)
            if m + 2 < G:
                wait(sp, s_af, n + 1)
                load_wo(m + 2)
            wait(dve, s_af, n + 1)
            if m == 0:
                wait(dve, s_st, NPAIR * G)
            s_mh.inc(dve.tensor_copy(MH[:, m, :], bank))
            wait(dve, s_mh, m + 1)
            s_ar.inc(dve.tensor_tensor(ML[:, m, :], bank, MH[:, m, :].bitcast(F32), ALU.subtract))
        return [(0.06 + 0.1 * m, lambda m=m: fold(m), 1.3) for m in range(G)]

    def scores(grp, par, s, h):
        qb, kt = STEPS[s]
        w = width(qb, kt)
        q0 = (qb + 1) * QB - w
        diagonal = kt * P >= qb * QB
        p = h // 2
        pair = NPAIR * grp + 2 * s + p
        if h % 2 == 0:
            wait(pe, s_p, pair + 1)
        if s == 0 and h == 0:
            wait(pe, s_nd, 16 * (grp + 2))
        ks = slice(kt * P, (kt + 1) * P)
        dst = PS[:, h, 0:w]
        pe.matmul(dst, KH[:, ks], Q[:, par, 0, h, q0:q0 + w], start=True, stop=False)
        pe.matmul(dst, KL[:, ks], Q[:, par, 0, h, q0:q0 + w], start=False, stop=False)
        ins = pe.matmul(dst, KH[:, ks], Q[:, par, 1, h, q0:q0 + w], start=False, stop=not diagonal)
        if diagonal:
            ins = pe.matmul(PS[:, h, 0:P], maskb[:], identb[:], start=False, stop=True)
        if h % 2:
            s_st.inc(ins)
            wait(act, s_st, NPAIR + pair + 1)
            if p == 0 and kt == 0:
                wait(act, s_rd, 4 * (2 * grp + qb) + 1)
            elif p == 0:
                j = ADDS.index(s)
                before = ADDS[j - 2] - (NSTEP if j < 2 else 0)
                wait(act, s_pv, 3 + NSTEP * grp + before + 1)
                wait(act, s_ad, NADD * grp + j + 1)
                wait(act, s_ae, NADD * grp + j + 1)
            s_p.inc(act.activation(slot(s)[:, 2 * p:2 * p + 2, 0:w], PS[:, 2 * p:2 * p + 2, 0:w], ACT.Exp))

    def slot(s):
        qb, kt = STEPS[s]
        return SUM[qb] if kt == 0 else PR[:, ADDS.index(s) % 2]

    def values(grp, s):
        qb, kt = STEPS[s]
        w = width(qb, kt)
        wait(pe, s_p, 2 + NPAIR * grp + 2 * s + 2)
        if kt == 0:
            wait(pe, s_o, 1 + 2 * grp + qb)
        for h in range(HG):
            ins = pe.matmul(PS[h * L:(h + 1) * L, 4, QB - w:QB], V[:, kt, :], slot(s)[:, h, 0:w],
                            start=(kt == 0), stop=(kt == (qb + 1) * QB // P - 1))
        s_pv.inc(ins)

    def add(grp, s, eng):
        qb, kt = STEPS[s]
        w = width(qb, kt)
        j = ADDS.index(s)
        done, heads = (s_ad, slice(0, POOL_HEADS)) if eng is pool else (s_ae, slice(POOL_HEADS, HG))
        wait(eng, s_p, 2 + NPAIR * grp + 2 * s + 2)
        if kt == 1:
            wait(eng, s_pv, 3 + NSTEP * grp + s)
        wait(eng, done, 2 + NADD * grp + j)
        sums = SUM[qb][:, heads, QB - w:QB]
        done.inc(eng.tensor_tensor(sums, sums, slot(s)[:, heads, 0:w], ALU.add))

    def denominator(side, grp, qb):
        n, bank = side.take()
        for done in (s_ad, s_ae):
            wait(pe, done, 2 + NADD * grp + (3 if qb == 0 else NADD))
        for h in range(HG):
            ins = pe.matmul(bank[h * L:(h + 1) * L, :], ones[:, 0:L], SUM[qb][:, h, :], start=True, stop=True)
        s_af.inc(ins)
        wait(dve, s_af, n + 1)
        wait(dve, s_no, 1 + 2 * grp + qb)
        s_ar.inc(dve.tensor_copy(RD[:], bank))
        copied[qb] = n

    copied, final = {}, {}

    def empty(grp, qb):
        wait(act, s_pv, 3 + NSTEP * grp + (4 if qb == 0 else NSTEP))
        s_o.inc(act.activation(out_of(grp, qb), PS[:, 4, :], ACT.Copy))

    def out_of(grp, qb):
        return attn[:, bass.ds(grp, 1), qb * QB:(qb + 1) * QB].rearrange("p g q -> p (g q)")

    def invert(grp, qb, n):
        wait(dve, s_ar, 3 + copied[qb] + 1)
        ap = RD[:, n * P:(n + 1) * P]
        s_rd.inc(dve.reciprocal(ap, ap))

    def normalise(grp, qb):
        wait(pool, s_o, 1 + 2 * grp + qb + 1)
        wait(pool, s_rd, 8 + 4 * (2 * grp + qb + 1))
        s_no.inc(pool.tensor_tensor(out_of(grp, qb), out_of(grp, qb), RD[:], ALU.mult))

    def floor_gate(gate):
        size, twice = cos[:, 0:D], cos[:, D:2 * D]
        s_gt.inc(dve.scalar_tensor_tensor(out=size, in0=gate[:], scalar=-1.0, in1=gate[:], op0=ALU.mult, op1=ALU.max))
        s_gt.inc(dve.tensor_scalar(twice, gate[:], 0.0, 2.0, ALU.is_ge, ALU.mult))
        wait(dve, s_gt, s_gt.n)
        s_gt.inc(dve.tensor_scalar(size, size, FLOOR, None, ALU.max))
        wait(dve, s_gt, s_gt.n)
        s_gt.inc(dve.scalar_tensor_tensor(out=gate[:], in0=twice, scalar=-1.0, in1=size, op0=ALU.add, op1=ALU.mult))
        wait(dve, s_gt, s_gt.n)

    def tiles_ready(qb):
        wait(pool, s_no, 1 + 2 * (G - 1) + qb + 1)
        pool.sem_inc(g("s_tiles").h, QB // P)

    def window(grp, par, with_maxima, with_queries):
        last = not with_maxima
        side = Side(U0 + UW * grp - (UQ if last else 0), U0 - (UQ if last else 0))
        work = []
        if last:
            work = fold_values(side) + [(0.3 + 0.3 * n, lambda gate=gate: floor_gate(gate), 2.5)
                                        for n, gate in enumerate((g("gate_a"), g("gate_b")))]
        if with_queries:
            wait(sp, s_wl, 1 + grp + 2)
            load_weights(grp + 2)
        if with_maxima:
            send_queries(grp + 1, 1 - par)
            work += maxima(side, grp + 1, 1 - par)
        if with_queries:
            work += queries(side, grp + 2)
        elif with_maxima:
            load_late()
        total = sum(width(*STEPS[s]) for s in range(NSTEP))
        place = free = 0.0

        def advance(cost, keep=None):
            nonlocal place, free
            place += cost / total
            work.sort(key=lambda x: x[0])
            while work and (len(work) > keep if keep is not None else max(work[0][0], free - SLACK) <= place):
                _, f, busy = work.pop(0)
                f()
                free = max(free, place) + busy / WINDOW_US

        for s in range(NSTEP + 1):
            if s < NSTEP:
                for h in range(HG):
                    scores(grp, par, s, h)
                    advance(3 * width(*STEPS[s]) / 16)
            if s > 0:
                if s == NSTEP:
                    advance(0, keep=1)
                values(grp, s - 1)
                if s - 1 in ADDS:
                    add(grp, s - 1, pool)
                    add(grp, s - 1, dve)
                    free = max(free, place) + ((HG - POOL_HEADS) * width(*STEPS[s - 1]) / 850 + 0.07) / WINDOW_US
                advance(width(*STEPS[s - 1]) / 8)
            if s == 4:
                empty(grp, 0)
                work.append((place + 0.04, lambda: denominator(side, grp, 0), 0.7))
                work += [(place + 0.04 + 0.03 * n, lambda n=n: invert(grp, 0, n), 0.9) for n in range(4)]
                work.append((place + 0.04 + 0.1, lambda: normalise(grp, 0), 0.0))
                if last:
                    work.append((place + 0.04 + 0.101, lambda: tiles_ready(0), 0.0))
        advance(0, keep=0)
        empty(grp, 1)
        denominator(side, grp, 1)
        final["side"] = 3 + side.first + side.at
        if not last:
            finish(grp)

    def finish(grp):
        for n in range(4):
            invert(grp, 1, n)
        normalise(grp, 1)

    def finish_last():
        finish(G - 1)
        tiles_ready(1)

    load_weights(0)
    first = Side(0, 0)
    columns = [(n, d) for n in (2, 3) for d in range(KD)]
    for _, f, _ in queries(first, 0, True):
        f()
        for n, d in columns[0:len(columns) > 4]:
            g("mod_columns")(n, d, PS[:, n - 2, 0:KD])
        columns = columns[1:] if len(columns) > 4 else columns
    for n, d in columns:
        g("mod_columns")(n, d, PS[:, n - 2, 0:KD])
    send_queries(0, 0)
    ahead = Side(UQ, UQ)
    wait(sp, s_wl, 2)
    load_weights(1)
    g("load_mod")(5)
    work = maxima(ahead, 0, 0) + [(place + 0.15, f, busy) for place, f, busy in queries(ahead, 1)]
    for n, gate in enumerate((g("gate_a"), g("gate_b"))):
        work += [(0.1 + 0.35 * n + 0.08 * k, lambda n=n, k=k, gate=gate: g("mod_rows")(4 + n, k, PS[:, 3 + n, :], gate), 0.0)
                 for k in range(KD)]
    for _, f, _ in sorted(work, key=lambda x: x[0]):
        f()
    wait(pe, g("s_mc"), 6)
    wait(act, g("s_mc"), 6)
    with nc.Fori(0, (G - 2) // 2) as i:
        window(2 * i, 0, True, True)
        window(2 * i + 1, 1, True, True)
    window(G - 2, 0, True, False)
    window(G - 1, 1, False, False)
    wait(sp, s_nd, 16 * (G + 1))
    return dict(values=(s_pv, 3 + NSTEP * G), blocks=(s_no, 1 + 2 * G), folded=(s_ar, final["side"]),
                finish=finish_last, sums=((s_ad, 2 + NADD * G), (s_ae, 2 + NADD * G)))


def phase_project(nc, t, c, sb, sem, wait, sh):
    pe, act, dve, pool, sp = nc.tensor, nc.scalar, nc.vector, nc.gpsimd, nc.sync
    g = lambda k: sh[k]
    PS, attn, gate_a, x1, h2H, h2L, MH, ML = map(g, ("PS", "attn", "gate_a", "x1", "h2H", "h2L", "MH", "ML"))
    stats, mv, rstd, eps, mod_col, ident, done = map(g, ("stats", "mv", "rstd", "eps", "mod_col", "ident", "done"))
    AH = sb("AH", [P, 2, G, P], F32R, c)
    AL = sb("AL", [P, 2, G, P], F32R, c)
    Y = sb("Y", [P, 2, D], F32, c)
    xn = sb("xn", [P, 2, D], F32, c)
    full = sb("full", [P, 2, KD, P], F32, c)
    s_ah = sem("s_ah")
    s_al = sem("s_al")
    s_y = sem("s_y")
    s_yr = sem("s_yr")
    s_yg = sem("s_yg")
    s_mv = sem("s_mv")
    s_sq = sem("s_sq")
    s_rs = sem("s_rs")
    s_xn = sem("s_xn")
    s_tr = sem("s_tr")
    s_full = sem("s_full")
    s_hi = sem("s_hi")
    s_lo = sem("s_lo")

    def load_chunk(ch, b, m_=P):
        for w, name in ((0, "gate_w"), (1, "up_w")):
            s_fw[b].inc(sp.dma_start(g("WI")[:, b, w, :, 0:m_], t[name][:, :, bass.ds(ch * P, m_)]), 16)
        s_fw[b].inc(sp.dma_start(g("DI")[0:m_, b, :], t["down_w"][bass.ds(ch * P, m_), :]), 16)

    s_fw = [sem("s_fw0"), sem("s_fw1")]
    for made in (done["values"], done["blocks"]) + done["sums"]:
        wait(sp, *made)
    for b in range(2):
        load_chunk(b, b)
    for made in (done["values"],) + done["sums"]:
        wait(act, *made)
    for e, s in ((pe, s_y), (pe, s_tr), (dve, s_yr), (pool, s_yg), (act, s_full), (pool, s_lo)):
        e.sem_inc(s.h, 2)
    wait(pe, *done["folded"])
    wait(pool, g("s_xr"), 16)

    def convert(st, b):
        src = attn[:, :, bass.ds(st * P, P)]
        wait(act, g("s_tiles"), st + 1)
        wait(act, s_y, st + 1)
        s_ah.inc(act.activation(AH[:, b], src, ACT.Copy))
        wait(dve, s_ah, st + 1)
        s_al.inc(dve.tensor_tensor(AL[:, b], src, AH[:, b].bitcast(F32), ALU.subtract))

    def products(st, b):
        wait(pe, s_al, st + 1)
        wait(pe, s_yr, st + 1)
        for n, (a, w) in enumerate(((AH, MH), (AL, MH), (AH, ML))):
            for grp in range(G):
                ins = pe.matmul(PS[:, b, :], a[:, b, grp, :], w[:, grp, :],
                                start=(n == 0 and grp == 0), stop=(n == 2 and grp == G - 1))
        s_y.inc(ins)

    def residual(st, b):
        wait(dve, s_y, 2 + st + 1)
        wait(dve, s_yg, st + 1)
        s_yr.inc(dve.tensor_tensor(Y[:, b], PS[:, b, :], gate_a[:], ALU.mult))
        wait(pool, s_yr, 2 + st + 1)
        s_yg.inc(pool.tensor_tensor(tile_of(st), tile_of(st), Y[:, b], ALU.add))

    def tile_of(st):
        return x1[:, bass.ds(st, 1), :].rearrange("p n d -> p (n d)")

    def normalise(st, b):
        wait(dve, s_yg, 2 + st + 1)
        s_mv.inc(dve.bn_stats(stats[:, b, :], tile_of(st)))
        wait(dve, s_mv, 2 * st + 1, alone=True)
        s_mv.inc(dve.bn_aggr(mv[:, b, :], stats[:, b, :]))
        wait(act, s_mv, 2 * st + 2)
        s_sq.inc(act.activation(rstd[:, b:b + 1], mv[:, b, 1:2], ACT.Sqrt, bias=eps[:, 1:2]))
        wait(dve, s_sq, st + 1)
        s_rs.inc(dve.reciprocal(rstd[:, b:b + 1], rstd[:, b:b + 1]))
        wait(dve, s_rs, st + 1)
        wait(dve, s_tr, st + 1)
        s_xn.inc(dve.tensor_scalar(xn[:, b, :], tile_of(st), mv[:, b, 0:1], rstd[:, b:b + 1], ALU.subtract, ALU.mult))

    def modulate(st, b):
        wait(pe, s_xn, st + 1)
        wait(pe, s_full, st + 1)
        for d in range(KD):
            ins = pe.transpose(PS[:, 2 + b, d * P:(d + 1) * P], xn[:, b, d * P:(d + 1) * P], ident[:])
        s_tr.inc(ins)
        wait(act, s_tr, 2 + st + 1)
        wait(act, s_lo, st + 1)
        for d in range(KD):
            ins = act.activation(full[:, b, d, :], PS[:, 2 + b, d * P:(d + 1) * P], ACT.Identity,
                                 scale=mod_col[:, 2, d:d + 1], bias=mod_col[:, 3, d:d + 1])
        s_full.inc(ins)
        cols = bass.ds(st * P, P)
        wait(dve, s_full, 2 + st + 1)
        s_hi.inc(dve.tensor_copy(h2H[:, :, cols], full[:, b]))
        wait(pool, s_hi, st + 1)
        s_lo.inc(pool.tensor_tensor(h2L[:, :, cols], full[:, b], h2H[:, :, cols].bitcast(F32), ALU.subtract))

    def step(st, b, first=False, last=False):
        if not last:
            convert(st + 1, 1 - b)
        products(st, b)
        residual(st, b)
        if not first:
            modulate(st - 1, 1 - b)
        if not last:
            normalise(st, b)

    convert(0, 0)
    done["finish"]()
    step(0, 0, first=True)
    with nc.Fori(0, (NS - 2) // 2) as i:
        step(2 * i + 1, 1)
        step(2 * i + 2, 0)
    step(NS - 1, 1, last=True)
    return dict(products=(s_y, 2 + NS), lo=s_lo, load_chunk=load_chunk, s_fw=s_fw,
                normalise=lambda: normalise(NS - 1, 1), modulate=lambda: modulate(NS - 1, 1))


def phase_ffn(nc, t, sb, sem, wait, sh, out):
    pe, act, dve, pool, sp = nc.tensor, nc.scalar, nc.vector, nc.gpsimd, nc.sync
    g = lambda k: sh[k]
    PS, gate_b, x1, h2H, h2L, ffn_s, WI, DI, Q, last = map(g, (
        "PS", "gate_b", "x1", "h2H", "h2L", "ffn_s", "WI", "DI", "Q", "last"))
    s_fw, load_chunk = last["s_fw"], last["load_chunk"]
    NCH = NC + 1
    hid = sh["wide"]
    DH = sb("DH", [P, NCH, D], F32R)
    DL = sb("DL", [P, NCH, D], F32R)
    WH, WL = [Q[:, 0, hl].rearrange("p h s -> p (h s)").rearrange("p (b w k m) -> p b w k m", b=2, w=2, k=KD) for hl in range(2)]
    SG = g("wo_slot")[:, 0, :]
    hid_last = g("wo_slot")[:, 1, :]
    s_h = sem("s_fh")
    s_l = sem("s_fl")
    s_dh = sem("s_fdh")
    s_dl = sem("s_fdl")
    s_g = sem("s_fg")
    s_u = sem("s_fu")
    s_sg = sem("s_fsg")
    s_hid = sem("s_fhid")
    dve.sem_inc(s_hid.h, 2)
    pe.sem_inc(s_u.h, 2)

    def prepare(ch, turn, b, m_=P):
        wait(act, s_fw[b], 48 * (turn + 1))
        wait(act, s_u, ch + 1)
        s_h.inc(act.activation(WH[:, b, :, :, 0:m_], WI[:, b, :, :, 0:m_], ACT.Copy))
        wait(dve, s_h, ch + 1)
        s_l.inc(dve.tensor_tensor(WL[:, b, :, :, 0:m_], WI[:, b, :, :, 0:m_], WH[:, b, :, :, 0:m_].bitcast(F32),
                                  ALU.subtract))

    def prepare_down(ch, b, m_=P):
        dh = DH[0:m_, bass.ds(ch, 1), :].rearrange("p c d -> p (c d)")
        dl = DL[0:m_, bass.ds(ch, 1), :].rearrange("p c d -> p (c d)")
        s_dh.inc(act.activation(dh, DI[0:m_, b, :], ACT.Copy))
        wait(dve, s_dh, ch + 1)
        s_dl.inc(dve.tensor_tensor(dl, DI[0:m_, b, :], dh.bitcast(F32), ALU.subtract))

    def gate_up(ch, b, m_=P):
        wait(pe, s_l, ch + 1)
        wait(pe, s_hid, ch + 1)
        first = isinstance(ch, int) and ch == 0
        for w, hf in ((0, 0), (1, 0), (0, 1), (1, 1)) if first else ((0, 0), (0, 1), (1, 0), (1, 1)):
            if first and w == 0:
                wait(pe, last["lo"], 2 + NS // 2 * (hf + 1))
            for n, (a, h) in enumerate(((WH, h2H), (WL, h2H), (WH, h2L))):
                for k in range(KD):
                    ins = pe.matmul(PS[0:m_, 4 * b + 2 * w + hf, :], a[:, b, w, k, 0:m_],
                                    h[:, k, hf * 512:(hf + 1) * 512],
                                    start=(n == 0 and k == 0), stop=(n == 2 and k == KD - 1))
            if hf == 1:
                (s_g, s_u)[w].inc(ins)
            if first and (w, hf) == (0, 0):
                last["modulate"]()
        wait(act, s_g, ch + 1)
        wait(act, s_hid, 2 + ch)
        s_sg.inc(act.activation(SG[0:m_, :].rearrange("p (b n) -> p b n", b=2), PS[0:m_, 4 * b:4 * b + 2, :], ACT.Silu,
                                scale=ffn_s[0:m_, 0:1]))
        wait(dve, s_sg, ch + 1)
        wait(dve, s_u, 2 + ch + 1)
        s_hid.inc(dve.scalar_tensor_tensor(
            out=hid[:, bass.ds(ch, 1), :].rearrange("p c s -> p (c s)") if m_ == P else hid_last[0:m_, :],
            in0=PS[0:m_, 4 * b + 2:4 * b + 4, :].rearrange("p b n -> p (b n)"), scalar=ffn_s[0:m_, 1:2],
            in1=SG[0:m_, :], op0=ALU.mult, op1=ALU.mult))

    def load_next(ch, b, m_=P):
        wait(sp, s_l, ch - 1)
        wait(sp, s_dl, ch - 1)
        load_chunk(ch, b, m_)

    wait(act, *last["products"])
    prepare(0, 0, 0)
    last["normalise"]()
    prepare(1, 0, 1)
    gate_up(0, 0)
    wait(act, last["lo"], 2 + NS)
    prepare_down(0, 0)
    with nc.Fori(0, (NC - 2) // 2) as i:
        load_next(2 * i + 2, 0)
        prepare(2 * i + 2, i + 1, 0)
        prepare_down(2 * i + 1, 1)
        gate_up(2 * i + 1, 1)
        load_next(2 * i + 3, 1)
        prepare(2 * i + 3, i + 1, 1)
        prepare_down(2 * i + 2, 0)
        gate_up(2 * i + 2, 0)
    load_next(NC, 0, IT)
    prepare(NC, NC // 2, 0, IT)
    prepare_down(NC - 1, 1)
    gate_up(NC - 1, 1)
    prepare_down(NC, 0, IT)

    def part(hl, b):
        whole = Q[:, b, hl].rearrange("p h s -> p (h s)")
        lo = whole.shape[1] // 2 if b == 0 else 0
        return whole[:, lo:lo + NCH * P].rearrange("p (c n) -> p c n", n=P)
    HH, HL = [part(0, b) for b in range(2)], [part(1, b) for b in range(2)]
    Y = sb("Y2", [P, 2, D])
    OT = sb("OT", [P, 2, D])
    s_hh = sem("s_hh")
    s_hl = sem("s_hl")
    s_y = sem("s_y2")
    s_yr = sem("s_yr2")
    s_ot = sem("s_ot")
    s_st = [sem("s_store0"), sem("s_store1")]
    for e, s in ((pe, s_y), (dve, s_yr), (pool, s_ot)):
        e.sem_inc(s.h, 2)
    for s in s_st:
        sp.sem_inc(s.h, 16)

    def convert(st, b, rest):
        if not rest:
            wait(act, s_y, st + 1)
            src, dst, dst_lo = hid[:, :, bass.ds(st * P, P)], HH[b][:, 0:NC, :], HL[b][:, 0:NC, :]
        else:
            src, dst, dst_lo = hid_last[0:IT, bass.ds(st * P, P)], HH[b][0:IT, NC, :], HL[b][0:IT, NC, :]
        s_hh.inc(act.activation(dst, src, ACT.Copy))
        wait(dve, s_hh, 2 * st + 1 + rest)
        s_hl.inc(dve.tensor_tensor(dst_lo, src, dst.bitcast(F32), ALU.subtract))

    def down(st, b):
        wait(pe, s_yr, st + 1)
        for rest, chunks in ((0, range(NC)), (1, (NC,))):
            wait(pe, s_hl, 2 * st + 1 + rest)
            k = IT if rest else P
            for n, (a, w) in enumerate(((HH, DH), (HL, DH), (HH, DL))):
                for ch in chunks:
                    ins = pe.matmul(PS[:, b, :], a[b][0:k, ch, :], w[0:k, ch, :],
                                    start=(n == 0 and ch == 0), stop=(n == 2 and rest == 1))
        s_y.inc(ins)

    def finish(st, i, b):
        wait(dve, s_y, 2 + st + 1)
        wait(dve, s_ot, st + 1)
        s_yr.inc(dve.scalar_tensor_tensor(out=Y[:, b], in0=PS[:, b, :], scalar=ffn_s[:, 2:3], in1=gate_b[:],
                                          op0=ALU.mult, op1=ALU.mult))
        wait(pool, s_yr, 2 + st + 1)
        wait(pool, s_st[b], 16 * (i + 1))
        s_ot.inc(pool.tensor_tensor(OT[:, b], x1[:, bass.ds(st, 1), :].rearrange("p n d -> p (n d)"), Y[:, b], ALU.add))
        wait(sp, s_ot, 2 + st + 1)
        s_st[b].inc(sp.dma_start(out[bass.ds(st * P, P), :], OT[:, b]), 16)

    wait(act, s_u, 2 + NC)
    wait(act, s_hid, 2 + NC)
    convert(0, 0, 0)
    gate_up(NC, 0, IT)
    wait(act, s_u, 2 + NCH)
    wait(act, s_hid, 2 + NCH)
    convert(0, 0, 1)
    wait(pe, s_hid, 2 + NCH)
    wait(pe, s_dl, NCH)
    with nc.Fori(0, NS // 2 - 1) as i:
        for b in range(2):
            for rest in range(2):
                convert(2 * i + b + 1, 1 - b, rest)
            down(2 * i + b, b)
            finish(2 * i + b, i, b)
    for rest in range(2):
        convert(NS - 1, 1, rest)
    for b in range(2):
        down(NS - 2 + b, b)
        finish(NS - 2 + b, NS // 2 - 1, b)
    for b in range(2):
        wait(sp, s_st[b], 16 * (NS // 2 + 1))
    nc.all_engine_barrier()


def rotary_tables():
    dim, base, factor, orig = 2 * HALF, 10000.0, 128.0, 1024

    def corr(r):
        return dim * math.log(orig / (r * 2 * math.pi)) / (2 * math.log(base))
    low, high = max(math.floor(corr(32.0)), 0), min(math.ceil(corr(1.0)), dim - 1)
    hi = high + 0.001 if low == high else float(high)
    ramp = np.clip((np.arange(dim // 2, dtype=np.float32) - low) / (hi - low), 0.0, 1.0)
    keep = 1.0 - ramp
    extra = 1.0 / base ** (np.arange(0, dim, 2, dtype=np.float32) / dim)
    inv = extra / factor * (1.0 - keep) + extra * keep
    freqs = np.outer(np.arange(S, dtype=np.float32), inv)
    return np.cos(freqs).astype(np.float32), np.sin(freqs).astype(np.float32)


def kernel(**inputs):
    import concourse.bacc as bacc
    from concourse.bass_utils import run_bass_kernel_spmd

    a = {k: np.asarray(v) for k, v in inputs.items()}
    cosT, sinT = (m.T for m in rotary_tables())
    wq = a["L0_attn_wq_b"].reshape(G, HG, NOPE + 2 * HALF, R)
    pe_rows = wq[:, :, NOPE:, :].reshape(G, HG, HALF, 2, R)
    wkv = a["L0_attn_wkv_b"].reshape(G, HG, NOPE + VD, L)
    ckv, kpe = a["L0_attn_wkv_a"][:L], a["L0_attn_wkv_a"][L:]
    wa = np.concatenate([a["L0_attn_wq_a"], kpe[0::2], kpe[1::2], ckv, kpe[1::2], kpe[0::2]], 0)
    chunks = lambda w: w.T.reshape(KD, P, -1).transpose(1, 0, 2)
    t = {
        "x": a["L0_attn_x"][0],
        "c": a["L0_c"].reshape(KD, P).T,
        "wmod": a["L0_wmod"].reshape(KD, P, 6, D).transpose(2, 1, 0, 3),
        "wa": chunks(wa),
        "lnq": a["L0_attn_q_a_ln_w"].reshape(R, 1),
        "lnkv": np.tile(a["L0_attn_kv_a_ln_w"], (P, 1)),
        "ffn_s": np.tile(np.concatenate([a["L0_ffn_gate_s"], a["L0_ffn_up_s"], a["L0_ffn_down_s"]]), (P, 1)),
        "cos": np.tile(cosT, (4, 1)),
        "sin": np.tile(sinT, (4, 1)),
        "rope_k": np.stack([np.concatenate([cosT, cosT]).T, np.concatenate([-sinT, sinT]).T], 1)
                  .reshape(NS, P, 2, 2 * HALF).transpose(1, 0, 2, 3),
        "wq_pe": pe_rows.transpose(0, 4, 3, 1, 2).reshape(G, R, 2 * P),
        "wq_nope": wq[:, :, :NOPE, :].transpose(0, 2, 1, 3).reshape(G, NOPE, HG * R),
        "wk": wkv[:, :, :NOPE, :].transpose(0, 2, 1, 3).reshape(G, NOPE, HG * L),
        "wv": wkv[:, :, NOPE:, :].transpose(2, 0, 1, 3).reshape(VD, G * HG * L),
        "wo": a["L0_attn_wo"].reshape(D, G, HG, VD).transpose(1, 3, 2, 0).reshape(G, VD, HG * D),
        "gate_w": chunks(a["L0_ffn_gate_w"]),
        "up_w": chunks(a["L0_ffn_up_w"]),
        "down_w": a["L0_ffn_down_w"].T,
    }
    nc = bacc.Bacc("TRN2", target_bir_lowering=False, num_devices=1)
    arrays, aps = {}, {}
    for name, v in t.items():
        v = np.ascontiguousarray(v)
        arrays["in_" + name] = v
        aps[name] = nc.dram_tensor("in_" + name, v.shape, mybir.dt.from_np(v.dtype), kind="ExternalInput").ap()
    out = nc.dram_tensor("out_0", (S, D), F32, kind="ExternalOutput").ap()
    build(nc, aps, out)
    r = run_bass_kernel_spmd(nc, [arrays], core_ids=[0])
    return r.results[0]["out_0"].reshape(1, S, D)
```
